# Optimizing a Trainium2 kernel written in Bass

```python
import numpy as np
import jax
import jax.numpy as jnp

def _softmax(x, axis=-1):
    return jax.nn.softmax(x, axis=axis)

def _gelu(x):
    return jax.nn.gelu(x, approximate=True)

def _silu(x):
    return jax.nn.silu(x)

def _sigmoid(x):
    return jax.nn.sigmoid(x)

def _layernorm(x, axis=-1, eps=1e-05):
    m = jnp.mean(x, axis=axis, keepdims=True)
    v = jnp.var(x, axis=axis, keepdims=True)
    return (x - m) / jnp.sqrt(v + eps)

def _scatter_add(tgt, idx, src, axis=0):
    return tgt.at[idx].add(src)

def _segment_sum(src, seg, n):
    return jax.ops.segment_sum(src, seg, n)
kernel_name = 'mk_decoder_preln_d1_seqx_r4_344046'

def setup_inputs(seed: int=0):
    np.random.seed(seed)
    _w = jnp.asarray

    def _rec_inputs():
        import jax
        import jax.numpy as jnp
        _rk = jax.random.key(seed)
        x = -0.000125 + 0.9999 * jax.random.normal(jax.random.fold_in(_rk, 1), (8, 512, 256), jnp.float32)
        _lenS = 512 - jax.random.randint(jax.random.fold_in(_rk, 7), (8,), 0, max(1, 512 // 4) + 1, jnp.int32)
        _lenS2 = 512 - jax.random.randint(jax.random.fold_in(_rk, 8), (8,), 0, max(1, 512 // 4) + 1, jnp.int32)
        _ctx_1024P = jax.random.normal(jax.random.fold_in(_rk, 11), (8, 16, 256), jnp.float32)
        _ctx_1024c = jax.random.dirichlet(jax.random.fold_in(_rk, 511), 0.3 * jnp.ones((16,), jnp.float32), (8, 512))
        _ctx_1024t = jnp.einsum('bsk,bkd->bsd', _ctx_1024c, _ctx_1024P)
        _ctx_1024t = _ctx_1024t * jax.lax.rsqrt(jnp.mean(jnp.square(_ctx_1024t)) + 1e-12) * 0.953939
        ctx_1024 = -1.52775e-05 + 0.999936 * (_ctx_1024t + 0.3 * jax.random.normal(jax.random.fold_in(_rk, 611), (8, 512, 256), jnp.float32))
        return (x, ctx_1024)
    x, ctx_1024 = _rec_inputs()

    def _L0_attn_setup():
        import jax, jax.numpy as jnp
        import numpy as np
        NUM_HEADS = 16
        key = jax.random.key(seed)
        ks = jax.random.split(key, 5)
        B, N, C = (2, 512, 256)
        x = jax.random.normal(ks[0], (B, N, C), dtype=jnp.float32)
        s_in = 1.0 / np.sqrt(C)
        Wq = jax.random.normal(ks[1], (C, 2 * C), dtype=jnp.float32) * s_in
        Wk = jax.random.normal(ks[2], (C, 2 * C), dtype=jnp.float32) * s_in
        Wv = jax.random.normal(ks[3], (C, 2 * C), dtype=jnp.float32) * s_in
        Wo = jax.random.normal(ks[4], (2 * C, C), dtype=jnp.float32) * (1.0 / np.sqrt(2 * C))
        return {'x': x, 'Wq': Wq, 'Wk': Wk, 'Wv': Wv, 'Wo': Wo}
    _L0_attn_all = _L0_attn_setup()
    _L0_attn_in = {k: v for k, v in _L0_attn_all.items() if k in ('Wq', 'Wk', 'Wv', 'Wo')}
    del _L0_attn_all

    def _L0_xattn_setup():
        import jax, jax.numpy as jnp
        import numpy as np
        import math
        NHEADS = 16
        CAUSAL = True
        NEG_INF = -1e+18
        key = jax.random.key(seed)
        kq, kk, kv = jax.random.split(key, 3)
        B, S, D = (4, 2048, 256)
        q = jax.random.normal(kq, (B, S, D), dtype=jnp.float32)
        k = jax.random.normal(kk, (B, S, D), dtype=jnp.float32)
        v = jax.random.normal(kv, (B, S, D), dtype=jnp.float32)
        return {'q': q, 'k': k, 'v': v}
    _L0_xattn_all = _L0_xattn_setup()
    _L0_xattn_in = {k: v for k, v in _L0_xattn_all.items() if k in ()}
    del _L0_xattn_all

    def _L0_ffn_setup():
        import jax, jax.numpy as jnp
        import numpy as np
        INT4_QMAX = 7.0

        def simulate_quantize_int4(w):
            scale = jnp.max(jnp.abs(w)) / INT4_QMAX
            q = jnp.clip(jnp.round(w / scale), -8.0, 7.0)
            return q * scale
        key = jax.random.key(seed)
        k_x, k_w, k_bias, k_a, k_b = jax.random.split(key, 5)
        d_in, features, rank = (256, 256, 16)
        x = jax.random.normal(k_x, (4, 2048, d_in), dtype=jnp.float32)
        kernel = jax.random.normal(k_w, (d_in, features), dtype=jnp.float32)
        bias = jax.random.normal(k_bias, (features,), dtype=jnp.float32)
        a = jax.random.normal(k_a, (d_in, rank), dtype=jnp.float32) * (1.0 / np.sqrt(d_in))
        b = jax.random.normal(k_b, (rank, features), dtype=jnp.float32) * 0.01
        return {'x': x, 'kernel': kernel, 'bias': bias, 'a': a, 'b': b}
    _L0_ffn_all = _L0_ffn_setup()
    _L0_ffn_in = {k: v for k, v in _L0_ffn_all.items() if k in ('kernel', 'bias', 'a', 'b')}
    del _L0_ffn_all
    return {'x': x, 'ctx_1024': ctx_1024, 'L0_attn_Wq': _L0_attn_in['Wq'], 'L0_attn_Wk': _L0_attn_in['Wk'], 'L0_attn_Wv': _L0_attn_in['Wv'], 'L0_attn_Wo': _L0_attn_in['Wo'], 'L0_ffn_kernel': _L0_ffn_in['kernel'], 'L0_ffn_bias': _L0_ffn_in['bias'], 'L0_ffn_a': _L0_ffn_in['a'], 'L0_ffn_b': _L0_ffn_in['b']}

def reference(x, ctx_1024, L0_attn_Wq, L0_attn_Wk, L0_attn_Wv, L0_attn_Wo, L0_ffn_kernel, L0_ffn_bias, L0_ffn_a, L0_ffn_b):
    import jax
    import jax.numpy as jnp

    def _L0_attn_ref(x, Wq, Wk, Wv, Wo):
        import jax, jax.numpy as jnp
        import numpy as np
        NUM_HEADS = 16
        B, N, C = x.shape
        H = NUM_HEADS
        hd = C // H

        def proj(W):
            return (x @ W).reshape(B, N, H, 2 * hd).transpose(0, 2, 1, 3)
        q = proj(Wq)
        k = proj(Wk)
        v = proj(Wv)
        q_r, q_i = (q[..., :hd], q[..., hd:])
        k_r, k_i = (k[..., :hd], k[..., hd:])
        v_r, v_i = (v[..., :hd], v[..., hd:])
        scores = (jnp.einsum('bhnd,bhmd->bhnm', q_r, k_r) + jnp.einsum('bhnd,bhmd->bhnm', q_i, k_i)) / jnp.sqrt(jnp.float32(hd))
        causal = jnp.tril(jnp.ones((N, N), dtype=bool))
        scores = jnp.where(causal[None, None], scores, -jnp.inf)
        probs = jax.nn.softmax(scores, axis=-1)
        out_r = jnp.einsum('bhnm,bhmd->bhnd', probs, v_r)
        out_i = jnp.einsum('bhnm,bhmd->bhnd', probs, v_i)
        out = jnp.concatenate([out_r, out_i], axis=-1)
        out = out.transpose(0, 2, 1, 3).reshape(B, N, 2 * C)
        return out @ Wo

    def _L0_xattn_ref(q, k, v):
        import jax, jax.numpy as jnp
        import numpy as np
        import math
        NHEADS = 16
        CAUSAL = True
        NEG_INF = -1e+18
        B, S, D = q.shape
        hd = D // NHEADS
        qh = q.reshape(B, S, NHEADS, hd)
        kh = k.reshape(B, S, NHEADS, hd)
        vh = v.reshape(B, S, NHEADS, hd)
        scores = jnp.einsum('bsqd,bskd->bsqk', qh, kh) / math.sqrt(hd)
        if CAUSAL:
            mask = jnp.tril(jnp.ones((NHEADS, NHEADS), dtype=bool))
            scores = jnp.where(mask, scores, jnp.asarray(NEG_INF, scores.dtype))
        attn = jax.nn.softmax(scores, axis=-1)
        out = jnp.einsum('bsqk,bskd->bsqd', attn, vh)
        return out.reshape(B, S, D)

    def _L0_ffn_ref(x, kernel, bias, a, b):
        import jax, jax.numpy as jnp
        import numpy as np
        INT4_QMAX = 7.0

        def simulate_quantize_int4(w):
            scale = jnp.max(jnp.abs(w)) / INT4_QMAX
            q = jnp.clip(jnp.round(w / scale), -8.0, 7.0)
            return q * scale
        w = simulate_quantize_int4(kernel)
        y = jnp.einsum('bsd,df->bsf', x, w) + bias
        lora = jnp.einsum('bsr,rf->bsf', jnp.einsum('bsd,dr->bsr', x, a), b)
        return y + lora
    x = x + _L0_attn_ref(_layernorm(x, axis=-1), L0_attn_Wq, L0_attn_Wk, L0_attn_Wv, L0_attn_Wo)
    x = x + _L0_xattn_ref(_layernorm(x, axis=-1), ctx_1024, ctx_1024)
    x = x + _L0_ffn_ref(_layernorm(x, axis=-1), L0_ffn_kernel, L0_ffn_bias, L0_ffn_a, L0_ffn_b)
    return x

_drawn_inputs = setup_inputs


def setup_inputs(seed=0):
    import zlib

    import numpy as np

    out = dict(_drawn_inputs(seed))
    spreads = {}
    factors = {'L0_ffn_a': 8.0, 'L0_ffn_b': 8.0}
    for name, (base, spread) in spreads.items():
        noise = np.random.default_rng([zlib.crc32(name.encode()), seed]).standard_normal(out[name].shape)
        drawn = base * np.exp(spread * noise) if base else spread * noise
        out[name] = jnp.asarray(drawn.astype(out[name].dtype))
    for name, factor in factors.items():
        out[name] = (out[name] * factor).astype(out[name].dtype)
    return out
```

```python
from contextlib import ExitStack

import concourse.bass as bass
from concourse import mybir

F32 = mybir.dt.float32
F32R = mybir.dt.float32r
BF16 = mybir.dt.bfloat16
ALU = mybir.AluOpType
ACT = mybir.ActivationFunctionType
AX_X = mybir.AxisListType.X

P = 128
MASKED = -1.0e30
EPS = 1e-5
QMAX = 7.0
ROUND = 1.5 * 2.0 ** 23


class Count:

    def __init__(self, turn, per_batch):
        self.turn, self.per_batch, self.total = turn, per_batch, 0

    def up(self, n=1):
        self.total += n
        return self.now()

    def now(self, back=0):
        value = self.total - back
        if self.turn.reg is None:
            return value
        assert value > 0
        return (self.turn.reg - self.turn.first) * self.per_batch + value


class Turn:

    def __init__(self):
        self.reg, self.first, self.counts = None, 0, []

    def count(self, per_batch):
        self.counts.append(Count(self, per_batch))
        return self.counts[-1]

    def batches(self, eng, body, n_batch):
        first, after = 3, n_batch - 2
        for i in range(-1, first):
            body(i, i)
        before = [c.total for c in self.counts]
        with eng.Fori(first, after) as reg:
            self.reg, self.first = reg, first
            body(first, reg)
        self.reg = None
        for c, was in zip(self.counts, before):
            assert c.total - was == c.per_batch, (c.total - was, c.per_batch)
            c.total += c.per_batch * (after - first - 1)
        for i in range(after, n_batch + 2):
            body(i, i)


def wait(eng, sem, value):
    if not isinstance(value, int) or value > 0:
        eng.wait_ge(sem, value)


def wait_apart(eng, long_past, *waits):
    for _, value in waits:
        if not isinstance(value, int):
            eng.compute_val(value)
    eng.wait_ge(long_past, 1)
    for sem, value in waits:
        wait(eng, sem, value)


def decoder_layer(nc, x, ctx_in, wq, wk, wv, wo, ffn_w, ffn_bias, ffn_a, ffn_b, out):
    N_BATCH, T, C = x.shape
    W = wq.shape[1]
    NH = 16
    D = W // NH
    HD = C // NH
    G = 4
    NG = NH // G
    NT = T // P
    CC = C // P
    RANK = ffn_a.shape[1]
    SLOTS = 4
    STACK = 3 * D
    SCALE = float(HD) ** -0.5
    assert D * G == P and D == 32 and NG == 4 and NT == 4 and CC == 2 and HD == 16 and T == 512
    UNITS = 10
    PTR = 4
    CHUNKS = NH // 4
    COFF = [4 * 4 * HD * (j * (j + 1) // 2) for j in range(CHUNKS + 1)]

    x_t = x.rearrange("b (t p) c -> b p t c", p=P)
    ctx_t = ctx_in.rearrange("b (t p) c -> b p t c", p=P)
    out_t = out.rearrange("b (t p) c -> b p t c", p=P)

    def ok(b):
        return 0 <= b < N_BATCH

    with ExitStack() as ctx:
        def sb(name, shape, dt=F32):
            return ctx.enter_context(nc.sbuf_tensor(name, shape, dt))

        def psum(name, shape, dt=F32):
            return ctx.enter_context(nc.psum_tensor(name, shape, dt))

        def sem(name):
            return ctx.enter_context(nc.semaphore(name))

        stack_q = sb("stack_q", [P, SLOTS, G, T], F32R)
        stack_k = sb("stack_k", [P, SLOTS, G, T], F32R)
        q_hi = sb("q_hi", [P, T], F32R)
        q_lo = sb("q_lo", [P, T], F32R)
        k_hi = sb("k_hi", [P, T], F32R)
        k_lo = sb("k_lo", [P, T], F32R)
        values = sb("values", [P, SLOTS, NT, P])
        probs = sb("probs", [P, PTR, T])
        xt_hi = sb("xt_hi", [P, CC, T], F32R)
        xt_lo = sb("xt_lo", [P, CC, T], F32R)
        w_hi = sb("w_hi", [P, CC, 3 * W], F32R)
        w_lo = sb("w_lo", [P, CC, 3 * W], F32R)
        wo_sb = sb("wo_sb", [P, NG, C])
        seg_max = sb("seg_max", [P, G, NT])
        neg_max = sb("neg_max", [P, 2, NT, G])
        max_row = sb("max_row", [G, 2, T], F32R)
        acc_sb = sb("acc_sb", [P, T])
        sum_sb = sb("sum_sb", [P, T])
        inv_sum = sb("inv_sum", [P, NT * G])
        attn_t = sb("attn_t", [P, NG, T])
        x_in = sb("x_in", [P, NT, C])
        x1 = sb("x1", [P, NT, C])
        x1n = sb("x1n", [P, NT, C])
        ctx_sb = sb("ctx_sb", [P, NT, C])
        x2 = sb("x2", [P, NT, C])
        x2n = sb("x2n", [P, NT, C])
        y_sb = sb("y_sb", [P, NT, C])
        x2t_hi = sb("x2t_hi", [P, CC, T], F32R)
        x2t_lo = sb("x2t_lo", [P, CC, T], F32R)
        wf_hi = sb("wf_hi", [P, CC, C], F32R)
        wf_lo = sb("wf_lo", [P, CC, C], F32R)
        prod = sb("prod", [P, 2, COFF[-1]])
        qk_prod, pv_prod = prod[:, 0, :], prod[:, 1, :]
        head_scores = sb("head_scores", [P, NH, NH])
        head_probs = sb("head_probs", [P, NH, NH])
        head_max = sb("head_max", [P, NH])
        head_sum = sb("head_sum", [P, NH])
        head_inv = sb("head_inv", [P, NH])
        head_out = sb("head_out", [P, C])
        ln_raw = sb("ln_raw", [P, 3, NT, 6])
        touched = sb("touched", [P, 3, 1])
        ln_mv = sb("ln_mv", [P, 3, NT, 2])
        ln_var = sb("ln_var", [P, 3, NT])
        ln_rstd = sb("ln_rstd", [P, 3, NT])
        ln_negm = sb("ln_negm", [P, 3, NT])
        ln_bias = sb("ln_bias", [P, 3, NT])
        ident = sb("ident", [P, P])
        pick = sb("pick", [P, G])
        ident_b = sb("ident_b", [P, P], BF16)
        mask_q = sb("mask_q", [P, P], BF16)
        mask_k = sb("mask_k", [P, P], BF16)
        ones = sb("ones", [P, P])
        minus_half, minus_one, eps = sb("minus_half", [P, NT]), sb("minus_one", [P, NT]), sb("eps", [P, NT])
        head_mask = sb("head_mask", [P, NH, NH], BF16)
        bias_bc = sb("bias_bc", [P, C])
        scal = sb("scal", [P, 8])
        flat = prod[:, :, :].rearrange("p a n -> p (a n)")
        w_raw = flat[:, 0:CC * 3 * W].rearrange("p (c n) -> p c n", c=CC)
        fw_raw = flat[:, CC * 3 * W:CC * 3 * W + CC * C].rearrange("p (c n) -> p c n", c=CC)
        fw_q = flat[:, CC * 3 * W + CC * C:CC * 3 * W + 2 * CC * C].rearrange("p (c n) -> p c n", c=CC)
        a_raw = x2n[:, 0, 0:CC * RANK].rearrange("p (c r) -> p c r", c=CC)
        a_t = x2n[0:RANK, 1, 0:C]
        b_raw = x2n[0:RANK, 2, 0:C]
        bias_row = x2n[0:1, 3, 0:C]
        max_line = x2[0:1, 0, 0:P]

        max_bank = [psum(f"max_bank{n}", [P, T]) for n in range(2)]
        exp_bank = [psum(f"exp_bank{n}", [P, T]) for n in range(2)]
        misc = [psum(f"misc{n}", [P, T]) for n in range(2)]
        acc_bank = psum("acc_bank", [P, T])
        sum_bank = psum("sum_bank", [P, T])

        w_loaded, wo_loaded, small_loaded = sem("w_loaded"), sem("wo_loaded"), sem("small_loaded")
        x_loaded, x1_loaded = sem("x_loaded"), sem("x1_loaded")
        ctx_loaded = [sem(f"ctx_loaded{t}") for t in range(NT)]
        const_ready, const_base = sem("const_ready"), sem("const_base")
        w_hi_ready, w_lo_ready = sem("w_hi_ready"), sem("w_lo_ready")
        wf_hi_ready, wf_ready = sem("wf_hi_ready"), sem("wf_ready")
        setup_pe, setup_dve, setup_act = sem("setup_pe"), sem("setup_dve"), sem("setup_act")
        ln_stats = [sem(f"ln{n}_stats") for n in range(3)]
        ln_scale = [sem(f"ln{n}_scale") for n in range(3)]
        ln_done = [sem(f"ln{n}_done") for n in range(3)]
        dve_own, pool_own = sem("dve_own"), sem("pool_own")
        xt_psum, xt_hi_ready, xt_ready = (sem("xt_psum"), sem("xt_hi_ready"), sem("xt_ready"))
        x2t_psum, x2t_hi_ready, x2t_ready = sem("x2t_psum"), sem("x2t_hi_ready"), sem("x2t_ready")
        qk_psum, qk_hi_ready, qk_lo_ready = sem("qk_psum"), sem("qk_hi_ready"), sem("qk_lo_ready")
        v_psum, v_ready = sem("v_psum"), sem("v_ready")
        stacked, max_stacked = sem("stacked"), sem("max_stacked")
        max_scored, max_taken, max_ready = sem("max_scored"), sem("max_taken"), sem("max_ready")
        max_psum, max_row_ready = sem("max_psum"), sem("max_row_ready")
        exp_scored, exp_done, pv_done = sem("exp_scored"), sem("exp_done"), sem("pv_done")
        acc_saved = sem("acc_saved")
        sums_psum, inv_ready, inv_psum, attn_ready = (sem("sums_psum"), sem("inv_ready"), sem("inv_psum"),
                                                      sem("attn_ready"))
        wo_psum = sem("wo_psum")
        y_psum, y_ready, y_stored = sem("y_psum"), sem("y_ready"), sem("y_stored")
        x1_added = sem("x1_added")
        hqk_prod, hqk_sum, h_masked, h_max, h_shifted = (sem("hqk_prod"), sem("hqk_sum"), sem("h_masked"),
                                                        sem("h_max"), sem("h_shifted"))
        h_exp, h_inv, hpv_prod, hpv_sum, h_out = (sem("h_exp"), sem("h_inv"), sem("hpv_prod"),
                                                  sem("hpv_sum"), sem("h_out"))
        x2_ready, x1_kept, yb_ready = sem("x2_ready"), sem("x1_kept"), sem("yb_ready")

        block = ctx.enter_context(nc.Block())

        def key_units():
            for h in range(G):
                yield [(h, 0, 0, T)], (0, 1, 0)
            for h in range(G):
                yield [(h, 1, 0, 3 * P), (h, 3, 3 * P, P)], (0, 2, 3 * P)
            for h in range(0, G, 2):
                yield [(h, 2, 0, 2 * P), (h + 1, 2, 2 * P, 2 * P)], (0, 2, 2 * P)

        def query_units():
            for h in range(G):
                yield [(h, 3, 0, T)], (3 * P, 1, 0)
            for h in range(G):
                yield [(h, 2, 0, 3 * P), (h, 0, 3 * P, P)], (2 * P, 2, P)
            for h in range(0, G, 2):
                yield [(h, 1, 0, 2 * P), (h + 1, 1, 2 * P, 2 * P)], (P, 2, 2 * P)

        KEY_UNITS, QUERY_UNITS = list(key_units()), list(query_units())
        assert len(KEY_UNITS) == len(QUERY_UNITS) == UNITS

        def stages(i, g):
            def group(ahead):
                b, n = divmod(g + ahead, NG)
                return (b, n) if ok(i + b) else None
            return {"C": group(0), "B": group(2), "A": group(3), "M": group(1), "N": group(-1)}

        def tiles(i, g):
            def tile(back):
                b, t = divmod(g - 1 - back, NT)
                b -= 1
                return (b, t) if ok(i + b) else None
            return tile(0), tile(1)

        @block.sync
        def _(sp):
            turn = Turn()
            n_x_used = turn.count(CC)
            n_lo = turn.count(2 * NG)
            n_free = turn.count(UNITS * NG)
            n_row = turn.count(NG)
            n_kept, n_x2 = turn.count(1), turn.count(NT)
            n_pv = turn.count(NT)
            n_y, n_stored = turn.count(CC), turn.count(16)

            sp.dma_start(x_in[:, :, :], x_t[0]).then_inc(x_loaded, 16)
            for n, w in enumerate((wq, wk, wv)):
                sp.dma_start(w_raw[:, :, n * W:(n + 1) * W],
                             w.rearrange("(c p) n -> p c n", p=P)).then_inc(w_loaded, 16)
            sp.dma_start(wo_sb[:, :, :], wo.rearrange("(g p) n -> p g n", p=P)).then_inc(wo_loaded, 16)
            sp.dma_start(fw_raw, ffn_w.rearrange("(c p) n -> p c n", p=P)).then_inc(small_loaded, 16)
            sp.dma_start(a_raw, ffn_a.rearrange("(c p) r -> p c r", p=P)).then_inc(small_loaded, 16)
            sp.dma_start(b_raw, ffn_b).then_inc(small_loaded, 16)
            sp.dma_start(bias_row, ffn_bias.rearrange("(o n) -> o n", o=1)).then_inc(small_loaded, 16)

            def body(i, b):
                for g in range(NG):
                    st = stages(i, g)
                    if g == 0 and ok(i - 1):
                        for t in (0, 1):
                            wait_apart(sp, const_ready, (hpv_prod, n_pv.up() - NT))
                            sp.dma_start(ctx_sb[:, t, :], ctx_t[b - 1, :, t, :]).then_inc(ctx_loaded[t], 16)
                    if g in (1, 2) and ok(i - 1):
                        t = g + 1
                        wait_apart(sp, const_ready, (hpv_prod, n_pv.up() - NT))
                        sp.dma_start(ctx_sb[:, t, :], ctx_t[b - 1, :, t, :]).then_inc(ctx_loaded[t], 16)
                    if g == 1 and ok(i + 2):
                        wait_apart(sp, const_ready, (xt_psum, n_x_used.up(CC)))
                        sp.dma_start(x_in[:, :, :], x_t[b + 2]).then_inc(x_loaded, 16)
                    if st["M"]:
                        sp.wait_ge(max_row_ready, n_row.up())
                        m_slot = st["M"][1]
                        sp.dma_start(stack_q[STACK:STACK + 1, m_slot, :, :].bitcast(F32),
                                     max_row[:, m_slot % 2, :].bitcast(F32)).then_inc(max_stacked, 16)
                    if st["A"]:
                        s = st["A"][1]
                        wait_apart(sp, const_ready, (qk_lo_ready, n_lo.up(2)),
                                   (exp_scored, n_free.up(UNITS) - UNITS * SLOTS))
                        for h in range(G):
                            for n, part in enumerate((q_hi, q_lo, q_hi)):
                                sp.dma_start(stack_q[n * D:(n + 1) * D, s, h, :].bitcast(F32),
                                             part[h * D:(h + 1) * D, :].bitcast(F32)).then_inc(stacked, 16)
                            for n, part in enumerate((k_hi, k_hi, k_lo)):
                                sp.dma_start(stack_k[n * D:(n + 1) * D, s, h, :].bitcast(F32),
                                             part[h * D:(h + 1) * D, :].bitcast(F32)).then_inc(stacked, 16)
                    if g == 0 and ok(i - 1):
                        if ok(i - 2):
                            wait_apart(sp, const_ready, (x1_kept, n_kept.up()), (x2_ready, n_x2.up(NT) - 1))
                        sp.dma_start(x1[:, :, :], x_t[b - 1]).then_inc(x1_loaded, 16)
                    if g == 3 and ok(i - 2):
                        wait_apart(sp, const_ready, (y_ready, n_y.up(CC)))
                        sp.dma_start(out_t[b - 2], y_sb[:, :, :]).then_inc(y_stored, 16)
                        n_stored.up(16)

            turn.batches(sp, body, N_BATCH)
            sp.wait_ge(y_stored, n_stored.now())

        @block.tensor
        def _(pe):
            turn = Turn()
            n_ln = [turn.count(1), None, turn.count(1)]
            r_lo, r_v, r_row, r_xt = turn.count(2 * NG), turn.count(NG), turn.count(NG), turn.count(CC)
            r_inv, r_attn, r_x1 = turn.count(NG), turn.count(NG), turn.count(CC)
            r_x2t, r_y = turn.count(CC), turn.count(CC)
            readers = [[], []]
            n_xt, n_x2t = turn.count(CC), turn.count(CC)
            n_stack, n_row = turn.count(16 * 6 * G * NG), turn.count(16 * NG)
            n_max_bank, n_max_ready = turn.count(UNITS * NG), turn.count(NG)
            n_exp_bank, n_probs, n_v = turn.count(UNITS * NG), turn.count(UNITS * NG), turn.count(NG)
            n_acc, n_sums, n_inv, n_attn = (turn.count(NG), turn.count(NG), turn.count(NG), turn.count(NG))

            def take(bank, reader, count):
                for s, c, total in readers[bank]:
                    wait(pe, s, c.now(c.total - total))
                count.up()
                readers[bank][:] = [(reader, count, count.total)]
                return misc[bank]

            def last_readers():
                for bank, last in enumerate((((v_ready, r_v), (inv_ready, r_inv), (y_ready, r_y)),
                                             ((max_row_ready, r_row), (attn_ready, r_attn), (y_ready, r_y)))):
                    readers[bank][:] = [(s, c, c.total) for s, c in last]

            def mm(*args, **kw):
                return nc.tensor.matmul(*args, **kw)

            def split_terms(a_hi, a_lo, b_hi, b_lo):
                return ((a_hi, b_hi), (a_hi, b_lo), (a_lo, b_hi))

            pe.wait_ge(const_ready, 1)
            pe.wait_ge(setup_dve, 1)
            nc.tensor.transpose(misc[0][0:1, 0:P], scal[:, 0:1], ident[:, :]).then_inc(setup_pe, 1)
            pe.wait_ge(small_loaded, 64)
            for c in range(CC):
                last = nc.tensor.transpose(misc[1][0:RANK, c * P:(c + 1) * P], a_raw[:, c, :], ident[:, :])
            last.then_inc(setup_pe, 1)
            pe.wait_ge(setup_dve, 2)
            mm(misc[0][:, 0:1], ones[0:1, 0:P], scal[0:1, 1:2], start=True, stop=True).then_inc(setup_pe, 1)
            pe.wait_ge(setup_act, 1)
            for c in range(CC):
                last = mm(misc[1][:, c * C:(c + 1) * C], a_t[:, c * P:(c + 1) * P], b_raw, start=True, stop=True)
            last.then_inc(setup_pe, 1)
            pe.wait_ge(setup_dve, 3)
            mm(misc[0][:, 0:C], ones[0:1, 0:P], bias_row, start=True, stop=True).then_inc(setup_pe, 1)
            pe.wait_ge(setup_act, 2)
            pe.wait_ge(wf_hi_ready, 1)

            def transpose_tokens(src, sem_out, c, reader, count):
                bank = take(c, reader, count)
                for t in range(NT):
                    last = nc.tensor.transpose(bank[:, t * P:(t + 1) * P], src[:, t, c * P:(c + 1) * P], ident[:, :])
                last.then_inc(sem_out, 1)

            def project_qk(g, which):
                bank = take(which, qk_lo_ready, r_lo)
                n = 0
                for c in range(CC):
                    for wpart, xpart in split_terms(w_hi, w_lo, xt_hi, xt_lo):
                        last = mm(bank[:, :], wpart[:, c, which * W + g * P:which * W + (g + 1) * P],
                                  xpart[:, c, :], start=(n == 0), stop=(n == 5))
                        n += 1
                last.then_inc(qk_psum, 1)

            def project_v(g):
                bank = take(0, v_ready, r_v)
                for t in range(NT):
                    n = 0
                    for c in range(CC):
                        for wpart, xpart in split_terms(w_hi, w_lo, xt_hi, xt_lo):
                            last = mm(bank[:, t * P:(t + 1) * P], xpart[:, c, t * P:(t + 1) * P],
                                      wpart[:, c, 2 * W + g * P:2 * W + (g + 1) * P],
                                      start=(n == 0), stop=(n == 5))
                            n += 1
                last.then_inc(v_psum, 1)

            def scores(bank, unit, lhs, rhs, slot, rows, key_side, done):
                parts, (col, count, step) = unit
                for n, (h, blk, at, width) in enumerate(parts):
                    first = blk * P if key_side else 0
                    mm(bank[:, at:at + width], lhs[0:rows, slot, h, blk * P:(blk + 1) * P],
                       rhs[0:rows, slot, h, first:first + width], start=(n == 0), stop=False,
                       skip_group_check=True)
                mask = mask_k if key_side else mask_q
                if count == 1:
                    o, m = bank[:, col:col + P], mask[:, :]
                else:
                    o = bank[:, :].rearrange("p (a n) -> p a n", n=P)[:, col // P:col // P + step // P + 1:step // P, :]
                    m = mask[:, None, :].to_broadcast([P, 2, P])
                mm(o, ident_b[:, :], m, start=False, stop=True, skip_group_check=True).then_inc(done, 1)

            def attend(units, slot, first_tile):
                pe.wait_ge(exp_done, n_probs.up(len(units)))
                rounds = [[], []]
                for n in units:
                    for k, (h, blk, at, width) in enumerate(KEY_UNITS[n][0]):
                        p = probs[:, (first_tile + n) % PTR, at:at + width]
                        rounds[k if len(units) > 1 else 0].append((h, blk, T - width, p))
                for r in rounds:
                    for h, blk, q0, p in r:
                        mm(acc_bank[h * D:(h + 1) * D, q0:T], values[:, slot, blk, h * D:(h + 1) * D], p,
                           start=(blk == 0), stop=(blk == 2), skip_group_check=True)
                    for h, blk, q0, p in r:
                        hs = (h + 2) % G
                        last = mm(sum_bank[hs * D:(hs + 1) * D, q0:T], ones[:, 0:D], p,
                                  start=(blk == 0), stop=(blk == 2), skip_group_check=True)
                last.then_inc(pv_done, len(units))

            def body(i, b):
                last_readers()
                for g in range(NG):
                    st = stages(i, g)
                    first_tile = UNITS * g
                    if st["C"]:
                        pe.wait_ge(max_stacked, n_row.up(16))
                    if st["B"]:
                        pe.wait_ge(stacked, n_stack.up(16 * 6 * G))
                    for n in range(UNITS):
                        if st["C"]:
                            wait(pe, exp_done, n_exp_bank.up() - 2)
                            scores(exp_bank[n % 2], KEY_UNITS[n], stack_k, stack_q, st["C"][1], STACK + 1,
                                   True, exp_scored)
                            if n == 2:
                                pe.wait_ge(v_ready, n_v.up())
                                wait(pe, acc_saved, n_acc.up() - 1)
                            if n in (2, 4, 6, 8):
                                attend((n - 2, n - 1), st["C"][1], first_tile)
                            if n == 9:
                                attend((8,), st["C"][1], first_tile)
                        if st["B"]:
                            wait(pe, max_taken, n_max_bank.up() - 2)
                            scores(max_bank[n % 2], QUERY_UNITS[n], stack_q, stack_k, st["B"][1], STACK,
                                   False, max_scored)
                        if st["A"] and n in (0, 1):
                            if n == 0 and st["A"][1] == 0:
                                pe.wait_ge(xt_ready, n_xt.up(CC))
                            project_qk(st["A"][1], n)
                        if st["A"] and n == 2:
                            project_v(st["A"][1])
                        if st["M"] and n == 3:
                            pe.wait_ge(max_ready, n_max_ready.up())
                            bank = take(1, max_row_ready, r_row)
                            for t in range(NT):
                                last = nc.tensor.transpose(bank[0:G, t * P:(t + 1) * P],
                                                           neg_max[:, st["M"][1] % 2, t, :], ident[:, :])
                            last.then_inc(max_psum, 1)
                        if g == 0 and ok(i + 1) and n in (4, 5):
                            if n == 4:
                                pe.wait_ge(ln_done[0], n_ln[0].up())
                            transpose_tokens(x_in, xt_psum, n - 4, xt_ready, r_xt)
                        if st["N"] and n == 5:
                            pe.wait_ge(acc_saved, n_sums.up())
                            bank = take(0, inv_ready, r_inv)
                            for t in range(NT):
                                last = mm(bank[:, t * G:(t + 1) * G], sum_sb[:, t * P:(t + 1) * P], pick[:, :],
                                          start=True, stop=True)
                            last.then_inc(sums_psum, 1)
                        if st["N"] and n == 7:
                            pe.wait_ge(inv_ready, n_inv.up())
                            bank = take(1, attn_ready, r_attn)
                            for t in range(NT):
                                last = nc.tensor.transpose(
                                    bank[:, t * P:(t + 1) * P],
                                    sum_sb[:, t * P:(t + 1) * P], ident[:, :])
                            last.then_inc(inv_psum, 1)
                        if g == 0 and ok(i - 1) and n == 9:
                            pe.wait_ge(attn_ready, n_attn.up(NG))
                            for half in range(2):
                                bank = take(half, x1_added, r_x1)
                                for t in range(2):
                                    for k in range(NG):
                                        last = mm(bank[:, t * C:(t + 1) * C],
                                                  attn_t[:, k, (2 * half + t) * P:(2 * half + t + 1) * P],
                                                  wo_sb[:, k, :], start=(k == 0), stop=(k == NG - 1))
                                last.then_inc(wo_psum, 1)
                        if g == 2 and ok(i - 2) and n in (8, 9):
                            if n == 8:
                                pe.wait_ge(ln_done[2], n_ln[2].up())
                            transpose_tokens(x2n, x2t_psum, n - 8, x2t_ready, r_x2t)
                        if g == 3 and ok(i - 2) and n in (8, 9):
                            if n == 8:
                                pe.wait_ge(x2t_ready, n_x2t.up(CC))
                            bank = take(n - 8, y_ready, r_y)
                            for t in range(2):
                                tok = (2 * (n - 8) + t) * P
                                k = 0
                                for c in range(CC):
                                    for xpart, wpart in split_terms(x2t_hi, x2t_lo, wf_hi, wf_lo):
                                        last = mm(bank[:, t * C:(t + 1) * C], xpart[:, c, tok:tok + P],
                                                  wpart[:, c, :], start=(k == 0), stop=(k == 5))
                                        k += 1
                            last.then_inc(y_psum, 1)
                    if st["C"]:
                        attend((9,), st["C"][1], first_tile)

            pe.wait_ge(w_lo_ready, 1)
            pe.wait_ge(wo_loaded, 16)
            pe.wait_ge(wf_ready, 1)
            turn.batches(pe, body, N_BATCH)

        @block.scalar
        def _(act):
            turn = Turn()
            n_ln = [turn.count(1), turn.count(1), turn.count(1)]
            n_xt, n_x2t, n_y = turn.count(CC), turn.count(CC), turn.count(CC)
            n_qk, n_staged = turn.count(2 * NG), turn.count(16 * 6 * G * NG)
            n_v, n_values = turn.count(NG), turn.count(UNITS * NG)
            n_row, n_row_free = turn.count(NG), turn.count(16 * NG)
            n_exp, n_saved, n_norm = turn.count(UNITS * NG), turn.count(UNITS * NG), turn.count(NG)
            n_x1n, n_shift = turn.count(NT), turn.count(NT)

            def copy(dst, src):
                return nc.scalar.activation(dst, src, ACT.Identity)

            act.wait_ge(w_loaded, 48)
            copy(w_hi[:, :, :], w_raw).then_inc(w_hi_ready, 1)
            act.wait_ge(setup_pe, 2)
            copy(a_t, misc[1][0:RANK, 0:C]).then_inc(setup_act, 1)
            act.wait_ge(setup_pe, 5)
            copy(bias_bc[:, :], misc[0][:, 0:C]).then_inc(setup_act, 1)

            def layernorm(which, src, dst):
                act.wait_ge(ln_scale[which], n_ln[which].up())
                for t in range(NT):
                    last = nc.scalar.activation(dst[:, t, :], src[:, t, :], ACT.Identity,
                                                bias=ln_bias[:, which, t:t + 1], scale=ln_rstd[:, which, t:t + 1])
                last.then_inc(ln_done[which], 1)

            def body(i, b):
                for g in range(NG):
                    st = stages(i, g)
                    now, then = tiles(i, g)
                    for n in range(UNITS):
                        if st["C"]:
                            act.wait_ge(exp_scored, n_exp.up())
                            wait(act, pv_done, n_exp.now(PTR) if turn.reg is not None or n_exp.total > PTR else 0)
                            nc.scalar.activation(probs[:, (UNITS * g + n) % PTR, :], exp_bank[n % 2][:, :],
                                                 ACT.Exp, scale=SCALE).then_inc(exp_done, 1)
                        if st["N"] and n == 0:
                            act.wait_ge(pv_done, n_saved.up(UNITS))
                            wait(act, attn_ready, n_norm.up() - 1)
                            copy(acc_sb[:, :], acc_bank[:, :])
                            copy(sum_sb[:, :], sum_bank[:, :]).then_inc(acc_saved, 1)
                        if st["A"] and n in (1, 2):
                            act.wait_ge(qk_psum, n_qk.up())
                            if n == 1:
                                wait(act, stacked, n_staged.up(16 * 6 * G) - 16 * 6 * G)
                            copy((q_hi, k_hi)[n - 1][:, :], misc[n - 1][:, :]).then_inc(qk_hi_ready, 1)
                        if g == 0 and ok(i + 1) and n == 2:
                            layernorm(0, x_in, x_in)
                        if g == 1 and ok(i - 1) and n == 2:
                            wait(act, hqk_prod, n_x1n.up(NT) - NT)
                            layernorm(1, x1, x1n)
                        if st["A"] and n == 3:
                            act.wait_ge(v_psum, n_v.up())
                            wait(act, pv_done, n_values.up(UNITS) - UNITS * SLOTS)
                            copy(values[:, st["A"][1], :, :].rearrange("p t n -> p (t n)"),
                                 misc[0][:, :]).then_inc(v_ready, 1)
                        if st["M"] and n == 4:
                            act.wait_ge(max_psum, n_row.up())
                            wait(act, max_stacked, n_row_free.up(16) - 32)
                            copy(max_row[:, st["M"][1] % 2, :], misc[1][0:G, :]).then_inc(max_row_ready, 1)
                        if g == 0 and ok(i + 1) and n in (5, 6):
                            act.wait_ge(xt_psum, n_xt.up())
                            copy(xt_hi[:, n - 5, :], misc[n - 5][:, :]).then_inc(xt_hi_ready, 1)
                        if g == 1 and ok(i - 2) and n == 9:
                            layernorm(2, x2, x2n)
                    if g == 2 and ok(i - 2):
                        wait(act, y_psum, n_y.up(CC) - CC)
                        for c in range(CC):
                            act.wait_ge(x2t_psum, n_x2t.up())
                            copy(x2t_hi[:, c, :], misc[c][:, :]).then_inc(x2t_hi_ready, 1)
                    if now:
                        act.wait_ge(h_shifted, n_shift.up())
                        nc.scalar.activation(head_probs[:, :, :], head_probs[:, :, :], ACT.Exp,
                                             scale=SCALE).then_inc(h_exp, 1)

            turn.batches(act, body, N_BATCH)

        @block.vector
        def _(dve):
            turn = Turn()
            n_own = turn.count(3 + NT + NG)
            n_x, n_x1 = turn.count(16), turn.count(16)
            n_scale = [turn.count(1), turn.count(1), turn.count(1)]
            n_hi, n_xt, n_x2t = turn.count(2 * NG), turn.count(CC), turn.count(CC)
            n_scored, n_row = turn.count(UNITS * NG), turn.count(NG)
            n_sums, n_inv = turn.count(NG), turn.count(NG)
            n_wo, n_y, n_yb = turn.count(CC), turn.count(CC), turn.count(1)
            n_prod, n_masked, n_exp = turn.count(NT), turn.count(NT), turn.count(NT)
            n_pv, n_kept, n_norm, n_ln2, n_yb2 = (turn.count(NT), turn.count(1), turn.count(NT), turn.count(1),
                                                 turn.count(1))

            def own(ins):
                ins.then_inc(dve_own, 1)
                dve.wait_ge(dve_own, n_own.up())

            def f32(ap):
                return ap.bitcast(F32)

            vec = nc.vector
            dve.wait_ge(small_loaded, 64)
            fw_flat = fw_raw.rearrange("p c n -> p (c n)")
            vec.tensor_reduce(scal[:, 0:1], fw_flat, axis=AX_X, op=ALU.max,
                              apply_absolute_value=True).then_inc(setup_dve, 1)
            dve.wait_ge(w_hi_ready, 1)
            vec.tensor_tensor(w_lo[:, :, :], w_raw, f32(w_hi[:, :, :]), ALU.subtract).then_inc(w_lo_ready, 1)
            dve.wait_ge(setup_pe, 1)
            vec.tensor_reduce(scal[0:1, 1:2], misc[0][0:1, 0:P], axis=AX_X, op=ALU.max).then_inc(setup_dve, 1)
            dve.wait_ge(setup_pe, 3)
            own(vec.tensor_scalar(scal[:, 2:3], misc[0][:, 0:1], 1.0 / QMAX, None, ALU.mult))
            vec.reciprocal(scal[:, 3:4], scal[:, 2:3]).then_inc(setup_dve, 1)
            dve.wait_ge(setup_dve, 3)
            own(vec.tensor_scalar(fw_q, fw_raw, scal[:, 3:4], None, ALU.mult))
            own(vec.tensor_scalar(fw_q, fw_q, ROUND, None, ALU.add))
            own(vec.tensor_scalar(fw_q, fw_q, -ROUND, None, ALU.add))
            own(vec.tensor_scalar(fw_q, fw_q, -QMAX - 1.0, QMAX, ALU.max, ALU.min))
            own(vec.tensor_scalar(fw_q, fw_q, scal[:, 2:3], None, ALU.mult))
            dve.wait_ge(setup_pe, 4)
            own(vec.tensor_tensor(fw_q, fw_q, misc[1][:, :].rearrange("p (c n) -> p c n", c=CC), ALU.add))
            vec.tensor_copy(wf_hi[:, :, :], fw_q).then_inc(wf_hi_ready, 1)
            dve.wait_ge(wf_hi_ready, 1)
            vec.tensor_tensor(wf_lo[:, :, :], fw_q, f32(wf_hi[:, :, :]), ALU.subtract).then_inc(wf_ready, 1)

            def ln_statistics(which, src):
                wait(dve, ln_scale[which], n_scale[which].up() - 1)
                for t in range(NT):
                    last = vec.bn_stats(ln_raw[:, which, t, :], src[:, t, :])
                last.then_inc(dve_own, 1)
                dve.wait_ge(dve_own, n_own.up())
                vec.tensor_copy(touched[:, which, :], ln_raw[:, which, 0, 0:1])
                for t in range(NT):
                    last = vec.bn_aggr(ln_mv[:, which, t, :], ln_raw[:, which, t, :])
                last.then_inc(ln_stats[which], 1)

            def take_max(n, ring):
                dve.wait_ge(max_scored, n_scored.up())
                bank = max_bank[n % 2]
                if n < G:
                    o, v = neg_max[:, ring, 3, n:n + 1], bank[:, :]
                elif n < 2 * G:
                    o, v = seg_max[:, n - G, :], bank[:, :].rearrange("p (s k) -> p s k", k=P)
                else:
                    h = 2 * (n - 2 * G)
                    o, v = neg_max[:, ring, 1, h:h + 2], bank[:, :].rearrange("p (s k) -> p s k", k=2 * P)
                vec.tensor_reduce(o, v, axis=AX_X, op=ALU.max, negate=True).then_inc(max_taken, 1)

            def body(i, b):
                for g in range(NG):
                    st = stages(i, g)
                    now, then = tiles(i, g)
                    for n in range(UNITS):
                        if st["B"]:
                            ring = st["B"][1] % 2
                            if n == 0:
                                wait(dve, max_psum, n_row.up() - 2)
                            take_max(n, ring)
                            if n == UNITS - 1:
                                dve.wait_ge(max_taken, n_scored.now())
                                vec.tensor_reduce(neg_max[:, ring, 2, :], seg_max[:, :, 0:3], axis=AX_X, op=ALU.min)
                                vec.tensor_copy(neg_max[:, ring, 0, :], seg_max[:, :, 3]).then_inc(max_ready, 1)
                        if n == 0 and then:
                            dve.wait_ge(h_exp, n_exp.up())
                            own(vec.tensor_reduce(head_sum[:, :], head_probs[:, :, :], axis=AX_X, op=ALU.add))
                            wait(dve, hpv_prod, n_norm.up() - 1)
                            vec.reciprocal(head_inv[:, :], head_sum[:, :]).then_inc(h_inv, 1)
                        if g == 0 and ok(i + 1) and n == 0:
                            dve.wait_ge(x_loaded, n_x.up(16))
                            ln_statistics(0, x_in)
                        if g == 1 and ok(i - 1) and n == 0:
                            dve.wait_ge(x1_loaded, n_x1.up(16))
                            for half in range(2):
                                dve.wait_ge(wo_psum, n_wo.up())
                                v = x1[:, 2 * half:2 * half + 2, :]
                                last = vec.tensor_tensor(v, v, misc[half][:, :].rearrange("p (t c) -> p t c", c=C), ALU.add)
                                last.then_inc(x1_added, 1)
                            dve.wait_ge(x1_added, n_wo.now())
                            ln_statistics(1, x1)
                        if st["A"] and n in (2, 3):
                            dve.wait_ge(qk_hi_ready, n_hi.up())
                            hi, lo = ((q_hi, q_lo), (k_hi, k_lo))[n - 2]
                            vec.tensor_tensor(lo[:, :], misc[n - 2][:, :], f32(hi[:, :]),
                                              ALU.subtract).then_inc(qk_lo_ready, 1)
                        if g == 0 and ok(i + 1) and n in (5, 6):
                            c = n - 5
                            dve.wait_ge(xt_hi_ready, n_xt.up())
                            vec.tensor_tensor(xt_lo[:, c, :], misc[c][:, :], f32(xt_hi[:, c, :]),
                                              ALU.subtract).then_inc(xt_ready, 1)
                        if then and n == 4:
                            dve.wait_ge(hpv_prod, n_pv.up())
                            for j in range(CHUNKS):
                                keys = 4 * (j + 1)
                                last = vec.tensor_reduce(
                                    head_out[:, j * 4 * HD:(j + 1) * 4 * HD],
                                    pv_prod[:, COFF[j]:COFF[j + 1]].rearrange("p (a k) -> p a k", k=keys),
                                    axis=AX_X, op=ALU.add)
                            last.then_inc(hpv_sum, 1)
                            dve.wait_ge(hpv_sum, n_pv.now())
                            t = then[1]
                            if t == 0:
                                wait(dve, ln_done[2], n_ln2.up() - 1)
                                wait(dve, yb_ready, n_yb2.up() - 1)
                            if t == NT - 1:
                                dve.wait_ge(x1_kept, n_kept.up())
                            src = x2 if t == NT - 1 else x1
                            vec.tensor_tensor(x2[:, t, :], src[:, t, :], head_out[:, :], ALU.add).then_inc(x2_ready, 1)
                        if g == 1 and ok(i - 2) and n == 5:
                            dve.wait_ge(x2_ready, n_pv.now())
                            ln_statistics(2, x2)
                        if st["N"] and n == 6:
                            dve.wait_ge(sums_psum, n_sums.up())
                            own(vec.reciprocal(inv_sum[:, :], misc[0][:, 0:NT * G]))
                            vec.tensor_copy(sum_sb[:, :].rearrange("p (a d) -> p a d", d=D),
                                            inv_sum[:, :, None].to_broadcast([P, NT * G, D])).then_inc(inv_ready, 1)
                        if st["N"] and n == 8:
                            dve.wait_ge(inv_psum, n_inv.up())
                            vec.tensor_tensor(attn_t[:, st["N"][1], :], acc_sb[:, :], misc[1][:, :],
                                              ALU.mult).then_inc(attn_ready, 1)
                        if now and n == 6:
                            dve.wait_ge(hqk_prod, n_prod.up())
                            wait(dve, h_masked, n_masked.up() - 1)
                            for j in range(CHUNKS):
                                keys = 4 * (j + 1)
                                last = vec.tensor_reduce(
                                    head_scores[:, 4 * j:4 * j + 4, 0:keys],
                                    qk_prod[:, COFF[j]:COFF[j + 1]].rearrange("p (q k d) -> p q k d", q=4, d=HD),
                                    axis=AX_X, op=ALU.add)
                            last.then_inc(hqk_sum, 1)
                        if now and n == 8:
                            dve.wait_ge(h_masked, n_masked.now())
                            vec.tensor_reduce(head_max[:, :], head_probs[:, :, :], axis=AX_X,
                                              op=ALU.max).then_inc(h_max, 1)
                    if g == 2 and ok(i - 2):
                        for c in range(CC):
                            dve.wait_ge(x2t_hi_ready, n_x2t.up())
                            vec.tensor_tensor(x2t_lo[:, c, :], misc[c][:, :], f32(x2t_hi[:, c, :]),
                                              ALU.subtract).then_inc(x2t_ready, 1)
                    if g == 3 and ok(i - 2):
                        dve.wait_ge(yb_ready, n_yb.up())
                        for half in range(2):
                            dve.wait_ge(y_psum, n_y.up())
                            v = y_sb[:, 2 * half:2 * half + 2, :]
                            vec.tensor_tensor(v, v, misc[half][:, :].rearrange("p (t c) -> p t c", c=C),
                                              ALU.add).then_inc(y_ready, 1)

            turn.batches(dve, body, N_BATCH)

        @block.gpsimd
        def _(pool):
            turn = Turn()
            n_own = turn.count(3 * 2 + NT)
            n_stats = [turn.count(1), turn.count(1), turn.count(1)]
            n_scaled = [turn.count(1), turn.count(1), turn.count(1)]
            n_x1n, n_kept_ln2 = turn.count(1), turn.count(1)
            n_ctx = [turn.count(16) for _ in range(NT)]
            n_qk, n_sum, n_max = turn.count(NT), turn.count(NT), turn.count(NT)
            n_inv, n_pv = turn.count(NT), turn.count(NT)
            n_x2, n_stored = turn.count(NT), turn.count(16)
            gp = nc.gpsimd

            def own(ins):
                ins.then_inc(pool_own, 1)
                pool.wait_ge(pool_own, n_own.up())

            gp.memset(ones[:, :], 1.0)
            gp.memset(ident[:, :], 0.0)
            gp.memset(mask_q[:, :], 0.0)
            gp.memset(mask_k[:, :], 0.0)
            gp.memset(head_mask[:, :, :], 0.0)
            gp.memset(minus_half[:, :], -0.5)
            gp.memset(minus_one[:, :], -1.0)
            gp.memset(eps[:, :], EPS)
            own(gp.memset(head_scores[:, :, :], 0.0))
            own(gp.memset(stack_k[STACK:STACK + 1, :, :, :].bitcast(F32), 1.0))
            own(gp.affine_select(out=ident[:, :], in_=ident[:, :], compare_op=ALU.not_equal, fill=1.0, base=0,
                                 pattern=[[-1, P]], channel_multiplier=1))
            gp.affine_select(out=mask_q[:, :], in_=mask_q[:, :], compare_op=ALU.is_ge, fill=MASKED, base=0,
                             pattern=[[-1, P]], channel_multiplier=1)
            gp.affine_select(out=mask_k[:, :], in_=mask_k[:, :], compare_op=ALU.is_ge, fill=MASKED, base=0,
                             pattern=[[1, P]], channel_multiplier=-1)
            gp.affine_select(out=head_mask[:, :, :], in_=head_mask[:, :, :], compare_op=ALU.is_ge, fill=MASKED,
                             base=0, pattern=[[1, NH], [-1, NH]], channel_multiplier=0)
            gp.tensor_copy(ident_b[:, :], ident[:, :])
            gp.tensor_copy(pick[:, 0:2], ident[:, 2 * D:P:D])
            gp.tensor_copy(pick[:, 2:4], ident[:, 0:2 * D:D]).then_inc(const_ready, 1)
            pool.wait_ge(const_ready, 1)

            def ln_coefficients(which):
                pool.wait_ge(ln_stats[which], n_stats[which].up())
                wait(pool, ln_done[which], n_scaled[which].up() - 1)
                own(gp.tensor_tensor(ln_var[:, which, :], ln_mv[:, which, :, 1], eps[:, :], ALU.add))
                gp.tensor_tensor(ln_negm[:, which, :], ln_mv[:, which, :, 0], minus_one[:, :], ALU.mult)
                own(gp.tensor_tensor(ln_rstd[:, which, :], ln_var[:, which, :], minus_half[:, :], ALU.pow))
                gp.tensor_tensor(ln_bias[:, which, :], ln_negm[:, which, :], ln_rstd[:, which, :],
                                 ALU.mult).then_inc(ln_scale[which], 1)

            def body(i, b):
                for g in range(NG):
                    now, then = tiles(i, g)
                    if g == 0 and ok(i + 1):
                        ln_coefficients(0)
                    if g == 1 and ok(i - 1):
                        ln_coefficients(1)
                    if then:
                        t = then[1]
                        pool.wait_ge(h_inv, n_inv.up())
                        own(gp.tensor_tensor(head_probs[:, :, :], head_probs[:, :, :],
                                             head_inv[:, :, None].to_broadcast([P, NH, NH]), ALU.mult))
                        wait(pool, hpv_sum, n_pv.up() - 1)
                        for j in range(CHUNKS):
                            keys = 4 * (j + 1)
                            last = gp.tensor_tensor(
                                pv_prod[:, COFF[j]:COFF[j + 1]].rearrange("p (q d k) -> p q d k", q=4, k=keys),
                                head_probs[:, 4 * j:4 * j + 4, None, 0:keys].to_broadcast([P, 4, HD, keys]),
                                ctx_sb[:, t, 0:keys * HD].rearrange("p (o k d) -> p o d k", o=1, d=HD)
                                .to_broadcast([P, 4, HD, keys]), ALU.mult)
                        last.then_inc(hpv_prod, 1)
                    if now:
                        t = now[1]
                        if t == 0:
                            pool.wait_ge(ln_done[1], n_x1n.up())
                        pool.wait_ge(ctx_loaded[t], n_ctx[t].up(16))
                        wait(pool, hqk_sum, n_qk.up() - 1)
                        for j in range(CHUNKS):
                            keys = 4 * (j + 1)
                            last = gp.tensor_tensor(
                                qk_prod[:, COFF[j]:COFF[j + 1]].rearrange("p (q k d) -> p q k d", q=4, d=HD),
                                x1n[:, t, 4 * j * HD:4 * (j + 1) * HD].rearrange("p (q o d) -> p q o d", o=1, d=HD)
                                .to_broadcast([P, 4, keys, HD]),
                                ctx_sb[:, t, 0:keys * HD].rearrange("p (o k d) -> p o k d", o=1, d=HD)
                                .to_broadcast([P, 4, keys, HD]), ALU.mult)
                        last.then_inc(hqk_prod, 1)
                        if t == NT - 1:
                            wait(pool, ln_done[2], n_kept_ln2.up() - 1)
                            gp.tensor_tensor(x2[:, t, :], x1[:, t, :], ones[:, 0:1].to_broadcast([P, C]), ALU.mult).then_inc(x1_kept, 1)
                    if g == 1 and ok(i - 2):
                        ln_coefficients(2)
                        pool.wait_ge(x2_ready, n_x2.up(NT))
                        wait(pool, y_stored, n_stored.up(16) - 16)
                        gp.tensor_tensor(y_sb[:, :, :], x2[:, :, :],
                                         bias_bc[:, None, :].to_broadcast([P, NT, C]), ALU.add).then_inc(yb_ready, 1)
                    if now:
                        pool.wait_ge(hqk_sum, n_sum.up())
                        gp.tensor_tensor(head_probs[:, :, :], head_scores[:, :, :], head_mask[:, :, :],
                                         ALU.add).then_inc(h_masked, 1)
                        pool.wait_ge(h_max, n_max.up())
                        gp.tensor_tensor(head_probs[:, :, :], head_probs[:, :, :],
                                         head_max[:, :, None].to_broadcast([P, NH, NH]),
                                         ALU.subtract).then_inc(h_shifted, 1)

            pool.wait_ge(w_lo_ready, 1)
            pool.wait_ge(wf_ready, 1)
            pool.wait_ge(setup_act, 2)
            turn.batches(pool, body, N_BATCH)

    return nc


INPUTS = ["x", "ctx_1024", "L0_attn_Wq", "L0_attn_Wk", "L0_attn_Wv", "L0_attn_Wo",
          "L0_ffn_kernel", "L0_ffn_bias", "L0_ffn_a", "L0_ffn_b"]


def kernel(**inputs):
    import numpy as np
    import concourse.bacc as bacc
    from concourse.bass_utils import run_bass_kernel_spmd

    nc = bacc.Bacc("TRN2", target_bir_lowering=False, num_devices=1)
    arrays, args = {}, []
    for name in INPUTS:
        a = np.ascontiguousarray(inputs[name])
        arrays[f"in_{name}"] = a
        args.append(nc.dram_tensor(f"in_{name}", a.shape, mybir.dt.from_np(a.dtype), kind="ExternalInput").ap())
    shape = inputs["x"].shape
    result = nc.dram_tensor("out_0", shape, F32, kind="ExternalOutput").ap()
    decoder_layer(nc, *args, result)
    r = run_bass_kernel_spmd(nc, [arrays], core_ids=[0])
    return r.results[0]["out_0"]
```

```python
from contextlib import ExitStack

import concourse.bass as bass
from concourse import mybir

F32 = mybir.dt.float32
F32R = mybir.dt.float32r
BF16 = mybir.dt.bfloat16
ALU = mybir.AluOpType
ACT = mybir.ActivationFunctionType
AX_X = mybir.AxisListType.X

P = 128
MASKED = -1.0e30
EPS = 1e-5
QMAX = 7.0
ROUND = 1.5 * 2.0 ** 23


class Count:

    def __init__(self, turn, per_batch):
        self.turn, self.per_batch, self.total = turn, per_batch, 0

    def up(self, n=1):
        self.total += n
        return self.now()

    def now(self, back=0):
        value = self.total - back
        if self.turn.reg is None:
            return value
        assert value > 0
        return (self.turn.reg - self.turn.first) * self.per_batch + value


class Turn:

    def __init__(self):
        self.reg, self.first, self.counts = None, 0, []

    def count(self, per_batch):
        self.counts.append(Count(self, per_batch))
        return self.counts[-1]

    def batches(self, eng, body, n_batch):
        first, after = 3, n_batch - 2
        for i in range(-1, first):
            body(i, i)
        before = [c.total for c in self.counts]
        with eng.Fori(first, after) as reg:
            self.reg, self.first = reg, first
            body(first, reg)
        self.reg = None
        for c, was in zip(self.counts, before):
            assert c.total - was == c.per_batch, (c.total - was, c.per_batch)
            c.total += c.per_batch * (after - first - 1)
        for i in range(after, n_batch + 3):
            body(i, i)


def wait(eng, sem, value):
    if not isinstance(value, int) or value > 0:
        eng.wait_ge(sem, value)


def wait_apart(eng, long_past, *waits):
    for _, value in waits:
        if not isinstance(value, int):
            eng.compute_val(value)
    eng.wait_ge(long_past, 1)
    for sem, value in waits:
        wait(eng, sem, value)


def decoder_layer(nc, x, ctx_in, wq, wk, wv, wo, ffn_w, ffn_bias, ffn_a, ffn_b, out):
    N_BATCH, T, C = x.shape
    W = wq.shape[1]
    NH = 16
    D = W // NH
    HD = C // NH
    G = 4
    NG = NH // G
    NT = T // P
    CC = C // P
    RANK = ffn_a.shape[1]
    SLOTS = 4
    STACK = 3 * D
    SCALE = float(HD) ** -0.5
    assert D * G == P and D == 32 and NG == 4 and NT == 4 and CC == 2 and HD == 16 and T == 512
    UNITS = 10
    LN_PARTS = 2
    STACK_DMAS = 6
    PTR = 4
    CHUNKS = NH // 4
    COFF = [4 * 4 * HD * (j * (j + 1) // 2) for j in range(CHUNKS + 1)]

    x_t = x.rearrange("b (t p) c -> b p t c", p=P)
    ctx_t = ctx_in.rearrange("b (t p) c -> b p t c", p=P)
    out_t = out.rearrange("b (t p) c -> b p t c", p=P)

    def ok(b):
        return 0 <= b < N_BATCH

    with ExitStack() as ctx:
        def sb(name, shape, dt=F32):
            return ctx.enter_context(nc.sbuf_tensor(name, shape, dt))

        def psum(name, shape, dt=F32):
            return ctx.enter_context(nc.psum_tensor(name, shape, dt))

        def sem(name):
            return ctx.enter_context(nc.semaphore(name))

        stack_q = sb("stack_q", [P, SLOTS, G, T], F32R)
        stack_k = sb("stack_k", [P, SLOTS, G, T], F32R)
        q_hi = sb("q_hi", [P, T], F32R)
        q_lo = sb("q_lo", [P, T], F32R)
        k_hi = sb("k_hi", [P, T], F32R)
        k_lo = sb("k_lo", [P, T], F32R)
        values = sb("values", [P, SLOTS, NT, P])
        probs = sb("probs", [P, PTR, T])
        xt_hi = sb("xt_hi", [P, CC, T], F32R)
        xt_lo = sb("xt_lo", [P, CC, T], F32R)
        w_hi = sb("w_hi", [P, CC, 3 * W], F32R)
        w_lo = sb("w_lo", [P, CC, 3 * W], F32R)
        wo_sb = sb("wo_sb", [P, NG, C])
        seg_max = sb("seg_max", [P, G, NT])
        neg_max = sb("neg_max", [P, 2, NT, G])
        max_row = sb("max_row", [G, 2, T], F32R)
        acc_sb = sb("acc_sb", [P, T])
        sum_sb = sb("sum_sb", [P, T])
        inv_sum = sb("inv_sum", [P, NT * G])
        attn_t = sb("attn_t", [P, NG, T])
        x_in = sb("x_in", [P, NT, C])
        x1 = sb("x1", [P, NT, C])
        x1n = sb("x1n", [P, NT, C])
        ctx_sb = sb("ctx_sb", [P, NT, C])
        x2 = sb("x2", [P, NT, C])
        x2n = sb("x2n", [P, NT, C])
        y_sb = sb("y_sb", [P, NT, C])
        x2t_hi = sb("x2t_hi", [P, CC, T], F32R)
        x2t_lo = sb("x2t_lo", [P, CC, T], F32R)
        wf_hi = sb("wf_hi", [P, CC, C], F32R)
        wf_lo = sb("wf_lo", [P, CC, C], F32R)
        prod = sb("prod", [P, 2, COFF[-1]])
        qk_prod, pv_prod = prod[:, 0, :], prod[:, 1, :]
        head_scores = sb("head_scores", [P, NH, NH])
        head_probs = sb("head_probs", [P, NH, NH])
        head_max = sb("head_max", [P, NH])
        head_sum = sb("head_sum", [P, NH])
        head_inv = sb("head_inv", [P, NH])
        head_out = sb("head_out", [P, C])
        ln_raw = sb("ln_raw", [P, 3, NT, 6])
        touched = sb("touched", [P, 3, 1])
        ln_mv = sb("ln_mv", [P, 3, NT, 2])
        ln_var = sb("ln_var", [P, 3, NT])
        ln_rstd = sb("ln_rstd", [P, 3, NT])
        ln_negm = sb("ln_negm", [P, 3, NT])
        ln_bias = sb("ln_bias", [P, 3, NT])
        ident = sb("ident", [P, P])
        pick = sb("pick", [P, G])
        ident_b = sb("ident_b", [P, P], BF16)
        mask_q = sb("mask_q", [P, P], BF16)
        mask_k = sb("mask_k", [P, P], BF16)
        ones = sb("ones", [P, P])
        minus_half, minus_one, eps = sb("minus_half", [P, NT]), sb("minus_one", [P, NT]), sb("eps", [P, NT])
        head_mask = sb("head_mask", [P, NH, NH], BF16)
        bias_bc = sb("bias_bc", [P, C])
        scal = sb("scal", [P, 8])
        flat = prod[:, :, :].rearrange("p a n -> p (a n)")
        w_raw = flat[:, 0:CC * 3 * W].rearrange("p (c n) -> p c n", c=CC)
        fw_raw = flat[:, CC * 3 * W:CC * 3 * W + CC * C].rearrange("p (c n) -> p c n", c=CC)
        fw_q = flat[:, CC * 3 * W + CC * C:CC * 3 * W + 2 * CC * C].rearrange("p (c n) -> p c n", c=CC)
        a_raw = x2n[:, 0, 0:CC * RANK].rearrange("p (c r) -> p c r", c=CC)
        a_t = x2n[0:RANK, 1, 0:C]
        b_raw = x2n[0:RANK, 2, 0:C]
        bias_row = x2n[0:1, 3, 0:C]
        max_line = x2[0:1, 0, 0:P]

        max_bank = [psum(f"max_bank{n}", [P, T]) for n in range(2)]
        exp_bank = [psum(f"exp_bank{n}", [P, T]) for n in range(2)]
        misc = [psum(f"misc{n}", [P, T]) for n in range(2)]
        acc_bank = psum("acc_bank", [P, T])
        sum_bank = psum("sum_bank", [P, T])

        w_loaded, wo_loaded, small_loaded = sem("w_loaded"), sem("wo_loaded"), sem("small_loaded")
        x_loaded, x1_loaded = sem("x_loaded"), sem("x1_loaded")
        ctx_loaded = [sem(f"ctx_loaded{t}") for t in range(NT)]
        const_ready, const_base = sem("const_ready"), sem("const_base")
        w_hi_ready, w_lo_ready = sem("w_hi_ready"), sem("w_lo_ready")
        wf_hi_ready, wf_ready = sem("wf_hi_ready"), sem("wf_ready")
        setup_pe, setup_dve, setup_act = sem("setup_pe"), sem("setup_dve"), sem("setup_act")
        ln_stats = [sem(f"ln{n}_stats") for n in range(3)]
        ln_scale = [sem(f"ln{n}_scale") for n in range(3)]
        ln_done = [sem(f"ln{n}_done") for n in range(3)]
        dve_own, pool_own = sem("dve_own"), sem("pool_own")
        xt_psum, xt_hi_ready, xt_ready = (sem("xt_psum"), sem("xt_hi_ready"), sem("xt_ready"))
        x2t_psum, x2t_hi_ready, x2t_ready = sem("x2t_psum"), sem("x2t_hi_ready"), sem("x2t_ready")
        qk_psum, qk_hi_ready, qk_lo_ready = sem("qk_psum"), sem("qk_hi_ready"), sem("qk_lo_ready")
        v_psum, v_ready = sem("v_psum"), sem("v_ready")
        stacked, max_stacked = sem("stacked"), sem("max_stacked")
        max_scored, max_taken, max_ready = sem("max_scored"), sem("max_taken"), sem("max_ready")
        max_psum, max_row_ready = sem("max_psum"), sem("max_row_ready")
        exp_scored, exp_done, pv_done = sem("exp_scored"), sem("exp_done"), sem("pv_done")
        acc_saved = sem("acc_saved")
        sums_psum, inv_ready, inv_psum, attn_ready = (sem("sums_psum"), sem("inv_ready"), sem("inv_psum"),
                                                      sem("attn_ready"))
        wo_psum = sem("wo_psum")
        y_psum, y_ready, y_stored = sem("y_psum"), sem("y_ready"), sem("y_stored")
        x1_added = sem("x1_added")
        hqk_prod, hqk_sum, h_masked, h_max, h_shifted = (sem("hqk_prod"), sem("hqk_sum"), sem("h_masked"),
                                                        sem("h_max"), sem("h_shifted"))
        h_exp, h_inv, hpv_prod, hpv_sum, h_out = (sem("h_exp"), sem("h_inv"), sem("hpv_prod"),
                                                  sem("hpv_sum"), sem("h_out"))
        x2_ready, x1_kept, yb_ready = sem("x2_ready"), sem("x1_kept"), sem("yb_ready")

        block = ctx.enter_context(nc.Block())

        def key_units():
            for h in range(G):
                yield [(h, 0, 0, T)], (0, 1, 0)
            for h in range(G):
                yield [(h, 1, 0, 3 * P), (h, 3, 3 * P, P)], (0, 2, 3 * P)
            for h in range(0, G, 2):
                yield [(h, 2, 0, 2 * P), (h + 1, 2, 2 * P, 2 * P)], (0, 2, 2 * P)

        def query_units():
            for h in range(G):
                yield [(h, 3, 0, T)], (3 * P, 1, 0)
            for h in range(G):
                yield [(h, 2, 0, 3 * P), (h, 0, 3 * P, P)], (2 * P, 2, P)
            for h in range(0, G, 2):
                yield [(h, 1, 0, 2 * P), (h + 1, 1, 2 * P, 2 * P)], (P, 2, 2 * P)

        KEY_UNITS, QUERY_UNITS = list(key_units()), list(query_units())
        assert len(KEY_UNITS) == len(QUERY_UNITS) == UNITS

        def stages(i, g):
            def group(ahead):
                b, n = divmod(g + ahead, NG)
                return (b, n) if ok(i + b) else None
            return {"C": group(0), "B": group(2), "A": group(3), "M": group(1), "N": group(-1)}

        def tiles(i, g):
            def tile(back):
                b, t = divmod(g - back, NT)
                return (b - 1, t) if ok(i + b - 1) else None
            return tile(2), tile(3), tile(4)

        def by_head(w, c):
            return w[:, c, 0:2 * W].rearrange("p (n h d) -> p n d h", h=G, d=D)

        def by_row(w, c):
            return w[:, c, 0:2 * W].rearrange("p (n d h) -> p n d h", h=G, d=D)

        @block.sync
        def _(sp):
            turn = Turn()
            n_x_used = turn.count(CC)
            n_lo = turn.count(2 * NG)
            n_free = turn.count(UNITS * NG)
            n_row = turn.count(NG)
            n_kept = turn.count(1)
            n_pv = turn.count(NT)
            n_y, n_stored = turn.count(CC), turn.count(16)

            sp.dma_start(x_in[:, :, :], x_t[0]).then_inc(x_loaded, 16)
            for n, w in enumerate((wq, wk, wv)):
                sp.dma_start(w_raw[:, :, n * W:(n + 1) * W],
                             w.rearrange("(c p) n -> p c n", p=P)).then_inc(w_loaded, 16)
            sp.dma_start(wo_sb[:, :, :], wo.rearrange("(g p) n -> p g n", p=P)).then_inc(wo_loaded, 16)
            sp.dma_start(fw_raw, ffn_w.rearrange("(c p) n -> p c n", p=P)).then_inc(small_loaded, 16)
            sp.dma_start(a_raw, ffn_a.rearrange("(c p) r -> p c r", p=P)).then_inc(small_loaded, 16)
            sp.dma_start(b_raw, ffn_b).then_inc(small_loaded, 16)
            sp.dma_start(bias_row, ffn_bias.rearrange("(o n) -> o n", o=1)).then_inc(small_loaded, 16)

            def body(i, b):
                for g in range(NG):
                    st = stages(i, g)
                    if g == 1 and ok(i + 2):
                        wait_apart(sp, const_ready, (xt_psum, n_x_used.up(CC)))
                        sp.dma_start(x_in[:, :, :], x_t[b + 2]).then_inc(x_loaded, 16)
                    if g == 3 and ok(i - 3):
                        wait_apart(sp, const_ready, (y_ready, n_y.up(CC)))
                        sp.dma_start(out_t[b - 3], y_sb[:, :, :]).then_inc(y_stored, 16)
                        n_stored.up(16)
                    if ok(i - 1):
                        wait_apart(sp, const_ready, (hpv_prod, n_pv.up() - NT))
                        sp.dma_start(ctx_sb[:, g, :], ctx_t[b - 1, :, g, :]).then_inc(ctx_loaded[g], 16)
                    if st["A"]:
                        s = st["A"][1]
                        wait_apart(sp, const_ready, (qk_lo_ready, n_lo.up(2)),
                                   (exp_scored, n_free.up(UNITS) - UNITS * SLOTS))
                        for stack, parts in ((stack_q, (q_hi, q_lo, q_hi)), (stack_k, (k_hi, k_hi, k_lo))):
                            for n, part in enumerate(parts):
                                sp.dma_start(stack[n * D:(n + 1) * D, s, :, :].bitcast(F32),
                                             part[:, :].bitcast(F32)).then_inc(stacked, 16)
                    if st["M"]:
                        sp.wait_ge(max_row_ready, n_row.up())
                        m_slot = st["M"][1]
                        sp.dma_start(stack_q[STACK:STACK + 1, m_slot, :, :].bitcast(F32),
                                     max_row[:, m_slot % 2, :].bitcast(F32)).then_inc(max_stacked, 16)
                    if g == 0 and ok(i - 1):
                        if ok(i - 2):
                            wait_apart(sp, const_ready, (x1_kept, n_kept.up()))
                        sp.dma_start(x1[:, :, :], x_t[b - 1]).then_inc(x1_loaded, 16)

            turn.batches(sp, body, N_BATCH)
            sp.wait_ge(y_stored, n_stored.now())

        @block.tensor
        def _(pe):
            turn = Turn()
            n_ln = [turn.count(LN_PARTS), None, turn.count(LN_PARTS)]
            r_lo, r_v, r_row, r_xt = turn.count(2 * NG), turn.count(NG), turn.count(NG), turn.count(CC)
            r_inv, r_attn, r_x1 = turn.count(NG), turn.count(NG), turn.count(CC)
            r_x2t, r_y = turn.count(CC), turn.count(CC)
            readers = [[], []]
            n_xt, n_x2t = turn.count(CC), turn.count(CC)
            n_stack, n_row = turn.count(16 * STACK_DMAS * NG), turn.count(16 * NG)
            n_max_bank, n_max_ready = turn.count(UNITS * NG), turn.count(NG)
            n_exp_bank, n_probs, n_v = turn.count(UNITS * NG), turn.count(UNITS * NG), turn.count(NG)
            n_acc, n_sums, n_inv, n_attn = (turn.count(NG), turn.count(NG), turn.count(NG), turn.count(NG))

            def take(bank, reader, count):
                for s, c, total in readers[bank]:
                    wait(pe, s, c.now(c.total - total))
                count.up()
                readers[bank][:] = [(reader, count, count.total)]
                return misc[bank]

            def last_readers():
                readers[0][:] = [(v_ready, r_v, r_v.total)]
                readers[1][:] = [(attn_ready, r_attn, r_attn.total)]

            def mm(*args, **kw):
                return nc.tensor.matmul(*args, **kw)

            def split_terms(a_hi, a_lo, b_hi, b_lo):
                return ((a_hi, b_hi), (a_hi, b_lo), (a_lo, b_hi))

            pe.wait_ge(const_ready, 1)
            pe.wait_ge(setup_dve, 1)
            nc.tensor.transpose(misc[0][0:1, 0:P], scal[:, 0:1], ident[:, :]).then_inc(setup_pe, 1)
            pe.wait_ge(small_loaded, 64)
            for c in range(CC):
                last = nc.tensor.transpose(misc[1][0:RANK, c * P:(c + 1) * P], a_raw[:, c, :], ident[:, :])
            last.then_inc(setup_pe, 1)
            pe.wait_ge(setup_dve, 2)
            mm(misc[0][:, 0:1], ones[0:1, 0:P], scal[0:1, 1:2], start=True, stop=True).then_inc(setup_pe, 1)
            pe.wait_ge(setup_act, 1)
            for c in range(CC):
                last = mm(misc[1][:, c * C:(c + 1) * C], a_t[:, c * P:(c + 1) * P], b_raw, start=True, stop=True)
            last.then_inc(setup_pe, 1)
            pe.wait_ge(setup_dve, 3)
            mm(misc[0][:, 0:C], ones[0:1, 0:P], bias_row, start=True, stop=True).then_inc(setup_pe, 1)
            pe.wait_ge(setup_act, 2)
            pe.wait_ge(wf_hi_ready, 1)

            def transpose_tokens(src, sem_out, c, reader, count):
                bank = take(c, reader, count)
                for t in range(NT):
                    last = nc.tensor.transpose(bank[:, t * P:(t + 1) * P], src[:, t, c * P:(c + 1) * P], ident[:, :])
                last.then_inc(sem_out, 1)

            def project_qk(g, which):
                bank = take(which, qk_lo_ready, r_lo)
                n = 0
                for c in range(CC):
                    for wpart, xpart in split_terms(w_hi, w_lo, xt_hi, xt_lo):
                        last = mm(bank[:, :], wpart[:, c, which * W + g * P:which * W + (g + 1) * P],
                                  xpart[:, c, :], start=(n == 0), stop=(n == 5))
                        n += 1
                last.then_inc(qk_psum, 1)

            def project_v(g):
                bank = take(0, v_ready, r_v)
                for t in range(NT):
                    n = 0
                    for c in range(CC):
                        for wpart, xpart in split_terms(w_hi, w_lo, xt_hi, xt_lo):
                            last = mm(bank[:, t * P:(t + 1) * P], xpart[:, c, t * P:(t + 1) * P],
                                      wpart[:, c, 2 * W + g * P:2 * W + (g + 1) * P],
                                      start=(n == 0), stop=(n == 5))
                            n += 1
                last.then_inc(v_psum, 1)

            def scores(bank, unit, lhs, rhs, slot, rows, key_side, done):
                parts, (col, count, step) = unit
                for n, (h, blk, at, width) in enumerate(parts):
                    first = blk * P if key_side else 0
                    mm(bank[:, at:at + width], lhs[0:rows, slot, h, blk * P:(blk + 1) * P],
                       rhs[0:rows, slot, h, first:first + width], start=(n == 0), stop=False,
                       skip_group_check=True)
                mask = mask_k if key_side else mask_q
                if count == 1:
                    o, m = bank[:, col:col + P], mask[:, :]
                else:
                    o = bank[:, :].rearrange("p (a n) -> p a n", n=P)[:, col // P:col // P + step // P + 1:step // P, :]
                    m = mask[:, None, :].to_broadcast([P, 2, P])
                mm(o, ident_b[:, :], m, start=False, stop=True, skip_group_check=True).then_inc(done, 1)

            def attend(units, slot, first_tile):
                pe.wait_ge(exp_done, n_probs.up(len(units)))
                rounds = [[], []]
                for n in units:
                    for k, (h, blk, at, width) in enumerate(KEY_UNITS[n][0]):
                        p = probs[:, (first_tile + n) % PTR, at:at + width]
                        rounds[k if len(units) > 1 else 0].append((h, blk, T - width, p))
                for r in rounds:
                    for h, blk, q0, p in r:
                        mm(acc_bank[h * D:(h + 1) * D, q0:T], values[:, slot, blk, h * D:(h + 1) * D], p,
                           start=(blk == 0), stop=(blk == 2), skip_group_check=True)
                    for h, blk, q0, p in r:
                        hs = (h + 2) % G
                        last = mm(sum_bank[hs * D:(hs + 1) * D, q0:T], ones[:, 0:D], p,
                                  start=(blk == 0), stop=(blk == 2), skip_group_check=True)
                last.then_inc(pv_done, len(units))

            def output_projection(half):
                bank = take(half, x1_added, r_x1)
                for t in range(2):
                    for k in range(NG):
                        last = mm(bank[:, t * C:(t + 1) * C],
                                  attn_t[:, k, (2 * half + t) * P:(2 * half + t + 1) * P],
                                  wo_sb[:, k, :], start=(k == 0), stop=(k == NG - 1))
                last.then_inc(wo_psum, 1)

            def ffn(half):
                bank = take(half, y_ready, r_y)
                for t in range(2):
                    tok = (2 * half + t) * P
                    k = 0
                    for c in range(CC):
                        for xpart, wpart in split_terms(x2t_hi, x2t_lo, wf_hi, wf_lo):
                            last = mm(bank[:, t * C:(t + 1) * C], xpart[:, c, tok:tok + P],
                                      wpart[:, c, :], start=(k == 0), stop=(k == 5))
                            k += 1
                last.then_inc(y_psum, 1)

            def body(i, b):
                if 1 <= i < N_BATCH:
                    last_readers()
                for g in range(NG):
                    st = stages(i, g)
                    first_tile = UNITS * g
                    if st["C"]:
                        pe.wait_ge(max_stacked, n_row.up(16))
                    if st["B"]:
                        pe.wait_ge(stacked, n_stack.up(16 * STACK_DMAS))
                    for n in range(UNITS):
                        if st["C"]:
                            wait(pe, exp_done, n_exp_bank.up() - 2)
                            scores(exp_bank[n % 2], KEY_UNITS[n], stack_k, stack_q, st["C"][1], STACK + 1,
                                   True, exp_scored)
                        if st["N"] and n == 0:
                            attend((8, 9), st["N"][1], first_tile - UNITS)
                        if st["C"]:
                            if n == 2:
                                pe.wait_ge(v_ready, n_v.up())
                                wait(pe, acc_saved, n_acc.up() - 1)
                            if n in (2, 4, 6, 8):
                                attend((n - 2, n - 1), st["C"][1], first_tile)
                        if st["B"]:
                            wait(pe, max_taken, n_max_bank.up() - 2)
                            scores(max_bank[n % 2], QUERY_UNITS[n], stack_q, stack_k, st["B"][1], STACK,
                                   False, max_scored)
                        if g == 1 and ok(i - 1) and n == 0:
                            output_projection(1)
                        if st["A"] and n in (1, 2):
                            if n == 1 and st["A"][1] == 0:
                                pe.wait_ge(xt_ready, n_xt.up(CC))
                            project_qk(st["A"][1], n - 1)
                        if st["N"] and n == 3:
                            pe.wait_ge(acc_saved, n_sums.up())
                            bank = take(0, inv_ready, r_inv)
                            for t in range(NT):
                                last = mm(bank[:, t * G:(t + 1) * G], sum_sb[:, t * P:(t + 1) * P], pick[:, :],
                                          start=True, stop=True)
                            last.then_inc(sums_psum, 1)
                        if st["M"] and n == 4:
                            pe.wait_ge(max_ready, n_max_ready.up())
                            bank = take(1, max_row_ready, r_row)
                            for t in range(NT):
                                last = nc.tensor.transpose(bank[0:G, t * P:(t + 1) * P],
                                                           neg_max[:, st["M"][1] % 2, t, :], ident[:, :])
                            last.then_inc(max_psum, 1)
                        if st["A"] and n == 5:
                            project_v(st["A"][1])
                        if st["N"] and n == 6:
                            pe.wait_ge(inv_ready, n_inv.up())
                            bank = take(1, attn_ready, r_attn)
                            for t in range(NT):
                                last = nc.tensor.transpose(
                                    bank[:, t * P:(t + 1) * P],
                                    sum_sb[:, t * P:(t + 1) * P], ident[:, :])
                            last.then_inc(inv_psum, 1)
                        if g == 0 and ok(i + 1) and n in (7, 8):
                            if n == 7:
                                pe.wait_ge(ln_done[0], n_ln[0].up(LN_PARTS))
                            transpose_tokens(x_in, xt_psum, n - 7, xt_ready, r_xt)
                        if g == 0 and ok(i - 1) and n == 9:
                            pe.wait_ge(attn_ready, n_attn.up(NG))
                            output_projection(0)
                        if g == 1 and ok(i - 3) and n in (7, 8):
                            if n == 7:
                                pe.wait_ge(ln_done[2], n_ln[2].up(LN_PARTS))
                            transpose_tokens(x2n, x2t_psum, n - 7, x2t_ready, r_x2t)
                        if g == 2 and ok(i - 3) and n in (7, 8):
                            if n == 7:
                                pe.wait_ge(x2t_ready, n_x2t.up(CC))
                            ffn(n - 7)

            pe.wait_ge(w_lo_ready, 1)
            pe.wait_ge(wo_loaded, 16)
            pe.wait_ge(wf_ready, 1)
            turn.batches(pe, body, N_BATCH)

        @block.scalar
        def _(act):
            turn = Turn()
            n_ln = [turn.count(1), turn.count(1), turn.count(1)]
            n_ln2 = turn.count(LN_PARTS)
            n_xt, n_x2t, n_yb = turn.count(CC), turn.count(CC), turn.count(1)
            n_qk, n_staged = turn.count(2 * NG), turn.count(16 * STACK_DMAS * NG)
            n_v, n_values = turn.count(NG), turn.count(UNITS * NG)
            n_row, n_row_free = turn.count(NG), turn.count(16 * NG)
            n_exp, n_saved, n_norm = turn.count(UNITS * NG), turn.count(UNITS * NG), turn.count(NG)
            n_x1n, n_shift = turn.count(NT), turn.count(NT)

            def copy(dst, src):
                return nc.scalar.activation(dst, src, ACT.Identity)

            act.wait_ge(w_loaded, 48)
            for c in range(CC):
                copy(by_row(w_hi, c), by_head(w_raw, c))
            copy(w_hi[:, :, 2 * W:], w_raw[:, :, 2 * W:]).then_inc(w_hi_ready, 1)
            act.wait_ge(setup_pe, 2)
            copy(a_t, misc[1][0:RANK, 0:C]).then_inc(setup_act, 1)
            act.wait_ge(setup_pe, 5)
            copy(bias_bc[:, :], misc[0][:, 0:C]).then_inc(setup_act, 1)

            def layernorm(which, src, dst, part):
                if part == 0:
                    act.wait_ge(ln_scale[which], n_ln[which].up())
                for t in (2 * part, 2 * part + 1):
                    last = nc.scalar.activation(dst[:, t, :], src[:, t, :], ACT.Identity,
                                                bias=ln_bias[:, which, t:t + 1], scale=ln_rstd[:, which, t:t + 1])
                last.then_inc(ln_done[which], 1)

            def body(i, b):
                for g in range(NG):
                    st = stages(i, g)
                    scored, attended, added = tiles(i, g)
                    for n in range(UNITS):
                        if st["C"]:
                            act.wait_ge(exp_scored, n_exp.up())
                            wait(act, pv_done, n_exp.now(PTR) if turn.reg is not None or n_exp.total > PTR else 0)
                            nc.scalar.activation(probs[:, (UNITS * g + n) % PTR, :], exp_bank[n % 2][:, :],
                                                 ACT.Exp, scale=SCALE).then_inc(exp_done, 1)
                        if attended and n == 0:
                            act.wait_ge(h_shifted, n_shift.up())
                            nc.scalar.activation(head_probs[:, :, :], head_probs[:, :, :], ACT.Exp,
                                                 scale=SCALE).then_inc(h_exp, 1)
                        if st["N"] and n == 1:
                            act.wait_ge(pv_done, n_saved.up(UNITS))
                            wait(act, attn_ready, n_norm.up() - 1)
                            copy(acc_sb[:, :], acc_bank[:, :])
                            copy(sum_sb[:, :], sum_bank[:, :]).then_inc(acc_saved, 1)
                        if st["A"] and n in (1, 2):
                            act.wait_ge(qk_psum, n_qk.up())
                            if n == 1:
                                wait(act, stacked, n_staged.up(16 * STACK_DMAS) - 16 * STACK_DMAS)
                            copy((q_hi, k_hi)[n - 1][:, :], misc[n - 1][:, :]).then_inc(qk_hi_ready, 1)
                        if g == 0 and ok(i - 3) and n in (2, 3):
                            layernorm(2, x2, x2n, n - 2)
                        if st["M"] and n == 4:
                            act.wait_ge(max_psum, n_row.up())
                            wait(act, max_stacked, n_row_free.up(16) - 32)
                            copy(max_row[:, st["M"][1] % 2, :], misc[1][0:G, :]).then_inc(max_row_ready, 1)
                        if st["A"] and n == 5:
                            act.wait_ge(v_psum, n_v.up())
                            wait(act, pv_done, n_values.up(UNITS) - UNITS * SLOTS)
                            copy(values[:, st["A"][1], :, :].rearrange("p t n -> p (t n)"),
                                 misc[0][:, :]).then_inc(v_ready, 1)
                        if g == 0 and ok(i + 1) and n in (5, 6):
                            layernorm(0, x_in, x_in, n - 5)
                        if g == 1 and ok(i - 1) and n in (5, 6):
                            if n == 5:
                                wait(act, hqk_prod, n_x1n.up(NT) - NT)
                            layernorm(1, x1, x1n, n - 5)
                        if g == 0 and ok(i + 1) and n in (7, 8):
                            act.wait_ge(xt_psum, n_xt.up())
                            copy(xt_hi[:, n - 7, :], misc[n - 7][:, :]).then_inc(xt_hi_ready, 1)
                        if g == 1 and ok(i - 3) and n in (7, 8):
                            act.wait_ge(x2t_psum, n_x2t.up())
                            copy(x2t_hi[:, n - 7, :], misc[n - 7][:, :]).then_inc(x2t_hi_ready, 1)
                        if g == 0 and ok(i - 2) and n == 4:
                            wait(act, yb_ready, n_yb.up() - 1)
                            wait(act, ln_done[2], n_ln2.up(LN_PARTS) - LN_PARTS)
                            copy(x2[:, :, :], x1[:, :, :]).then_inc(x1_kept, 1)

            turn.batches(act, body, N_BATCH)

        @block.vector
        def _(dve):
            turn = Turn()
            n_own = turn.count(3 + NT + NG)
            n_x, n_x1 = turn.count(16), turn.count(16)
            n_scale = [turn.count(1), turn.count(1), turn.count(1)]
            n_hi, n_xt, n_x2t = turn.count(2 * NG), turn.count(CC), turn.count(CC)
            n_scored, n_row = turn.count(UNITS * NG), turn.count(NG)
            n_sums, n_inv = turn.count(NG), turn.count(NG)
            n_wo, n_y, n_yb = turn.count(CC), turn.count(CC), turn.count(1)
            n_prod, n_masked, n_exp = turn.count(NT), turn.count(NT), turn.count(NT)
            n_pv, n_kept, n_norm = turn.count(NT), turn.count(1), turn.count(NT)

            def own(ins):
                ins.then_inc(dve_own, 1)
                dve.wait_ge(dve_own, n_own.up())

            def f32(ap):
                return ap.bitcast(F32)

            vec = nc.vector
            dve.wait_ge(small_loaded, 64)
            fw_flat = fw_raw.rearrange("p c n -> p (c n)")
            vec.tensor_reduce(scal[:, 0:1], fw_flat, axis=AX_X, op=ALU.max,
                              apply_absolute_value=True).then_inc(setup_dve, 1)
            dve.wait_ge(w_hi_ready, 1)
            for c in range(CC):
                vec.tensor_tensor(by_row(w_lo, c), by_head(w_raw, c), f32(by_row(w_hi, c)), ALU.subtract)
            vec.tensor_tensor(w_lo[:, :, 2 * W:], w_raw[:, :, 2 * W:], f32(w_hi[:, :, 2 * W:]),
                              ALU.subtract).then_inc(w_lo_ready, 1)
            dve.wait_ge(setup_pe, 1)
            vec.tensor_reduce(scal[0:1, 1:2], misc[0][0:1, 0:P], axis=AX_X, op=ALU.max).then_inc(setup_dve, 1)
            dve.wait_ge(setup_pe, 3)
            own(vec.tensor_scalar(scal[:, 2:3], misc[0][:, 0:1], 1.0 / QMAX, None, ALU.mult))
            vec.reciprocal(scal[:, 3:4], scal[:, 2:3]).then_inc(setup_dve, 1)
            dve.wait_ge(setup_dve, 3)
            own(vec.tensor_scalar(fw_q, fw_raw, scal[:, 3:4], None, ALU.mult))
            own(vec.tensor_scalar(fw_q, fw_q, ROUND, None, ALU.add))
            own(vec.tensor_scalar(fw_q, fw_q, -ROUND, None, ALU.add))
            own(vec.tensor_scalar(fw_q, fw_q, -QMAX - 1.0, QMAX, ALU.max, ALU.min))
            own(vec.tensor_scalar(fw_q, fw_q, scal[:, 2:3], None, ALU.mult))
            dve.wait_ge(setup_pe, 4)
            own(vec.tensor_tensor(fw_q, fw_q, misc[1][:, :].rearrange("p (c n) -> p c n", c=CC), ALU.add))
            vec.tensor_copy(wf_hi[:, :, :], fw_q).then_inc(wf_hi_ready, 1)
            dve.wait_ge(wf_hi_ready, 1)
            vec.tensor_tensor(wf_lo[:, :, :], fw_q, f32(wf_hi[:, :, :]), ALU.subtract).then_inc(wf_ready, 1)

            def ln_statistics(which, src):
                wait(dve, ln_scale[which], n_scale[which].up() - 1)
                for t in range(NT):
                    last = vec.bn_stats(ln_raw[:, which, t, :], src[:, t, :])
                last.then_inc(dve_own, 1)
                dve.wait_ge(dve_own, n_own.up())
                vec.tensor_copy(touched[:, which, :], ln_raw[:, which, 0, 0:1])
                for t in range(NT):
                    last = vec.bn_aggr(ln_mv[:, which, t, :], ln_raw[:, which, t, :])
                last.then_inc(ln_stats[which], 1)

            def take_max(n, ring):
                dve.wait_ge(max_scored, n_scored.up())
                bank = max_bank[n % 2]
                if n < G:
                    o, v = neg_max[:, ring, 3, n:n + 1], bank[:, :]
                elif n < 2 * G:
                    o, v = seg_max[:, n - G, :], bank[:, :].rearrange("p (s k) -> p s k", k=P)
                else:
                    h = 2 * (n - 2 * G)
                    o, v = neg_max[:, ring, 1, h:h + 2], bank[:, :].rearrange("p (s k) -> p s k", k=2 * P)
                vec.tensor_reduce(o, v, axis=AX_X, op=ALU.max, negate=True).then_inc(max_taken, 1)

            def sum_products(out, products, chunks):
                for j in chunks:
                    last = vec.tensor_reduce(out(j), products(j), axis=AX_X, op=ALU.add)
                return last

            def score_sums(chunks):
                return sum_products(
                    lambda j: head_scores[:, 4 * j:4 * j + 4, 0:4 * (j + 1)],
                    lambda j: qk_prod[:, COFF[j]:COFF[j + 1]].rearrange("p (q k d) -> p q k d", q=4, d=HD), chunks)

            def value_sums(chunks):
                return sum_products(
                    lambda j: head_out[:, j * 4 * HD:(j + 1) * 4 * HD],
                    lambda j: pv_prod[:, COFF[j]:COFF[j + 1]].rearrange("p (a k) -> p a k", k=4 * (j + 1)), chunks)

            def add_to_x1(half):
                dve.wait_ge(wo_psum, n_wo.up())
                v = x1[:, 2 * half:2 * half + 2, :]
                vec.tensor_tensor(v, v, misc[half][:, :].rearrange("p (t c) -> p t c", c=C),
                                  ALU.add).then_inc(x1_added, 1)

            def body(i, b):
                for g in range(NG):
                    st = stages(i, g)
                    scored, attended, added = tiles(i, g)
                    for n in range(UNITS):
                        if st["B"]:
                            ring = st["B"][1] % 2
                            if n == 0:
                                wait(dve, max_psum, n_row.up() - 2)
                            take_max(n, ring)
                            if n == UNITS - 1:
                                dve.wait_ge(max_taken, n_scored.now())
                                vec.tensor_reduce(neg_max[:, ring, 2, :], seg_max[:, :, 0:3], axis=AX_X, op=ALU.min)
                                vec.tensor_copy(neg_max[:, ring, 0, :], seg_max[:, :, 3]).then_inc(max_ready, 1)
                        if g == 1 and ok(i - 1) and n == 0:
                            dve.wait_ge(x1_loaded, n_x1.up(16))
                            add_to_x1(0)
                        if added and n == 0:
                            dve.wait_ge(hpv_prod, n_pv.up())
                            wait(dve, x2_ready, n_pv.now(1))
                            value_sums((3,))
                        if g == 0 and ok(i + 1) and n == 1:
                            dve.wait_ge(x_loaded, n_x.up(16))
                            ln_statistics(0, x_in)
                        if g == 1 and ok(i - 1) and n == 1:
                            add_to_x1(1)
                            dve.wait_ge(x1_added, n_wo.now())
                            ln_statistics(1, x1)
                        if st["A"] and n in (2, 3):
                            dve.wait_ge(qk_hi_ready, n_hi.up())
                            hi, lo = ((q_hi, q_lo), (k_hi, k_lo))[n - 2]
                            vec.tensor_tensor(lo[:, :], misc[n - 2][:, :], f32(hi[:, :]),
                                              ALU.subtract).then_inc(qk_lo_ready, 1)
                        if attended and n == 2:
                            dve.wait_ge(h_exp, n_exp.up())
                            own(vec.tensor_reduce(head_sum[:, :], head_probs[:, :, :], axis=AX_X, op=ALU.add))
                            wait(dve, hpv_prod, n_norm.up() - 1)
                            vec.reciprocal(head_inv[:, :], head_sum[:, :]).then_inc(h_inv, 1)
                        if added and n == 1:
                            value_sums((2,))
                        if added and n == 2:
                            value_sums((0, 1)).then_inc(hpv_sum, 1)
                        if st["N"] and n == 4:
                            dve.wait_ge(sums_psum, n_sums.up())
                            own(vec.reciprocal(inv_sum[:, :], misc[0][:, 0:NT * G]))
                            vec.tensor_copy(sum_sb[:, :].rearrange("p (a d) -> p a d", d=D),
                                            inv_sum[:, :, None].to_broadcast([P, NT * G, D])).then_inc(inv_ready, 1)
                        if added and n == 5:
                            t = added[1]
                            if t == 0:
                                dve.wait_ge(x1_kept, n_kept.up())
                            dve.wait_ge(hpv_sum, n_pv.now())
                            vec.tensor_tensor(x2[:, t, :], x2[:, t, :], head_out[:, :], ALU.add).then_inc(x2_ready, 1)
                            if t == NT - 1:
                                dve.wait_ge(x2_ready, n_pv.now())
                                ln_statistics(2, x2)
                        if scored and n == 5:
                            dve.wait_ge(hqk_prod, n_prod.up())
                            wait(dve, h_masked, n_masked.up() - 1)
                            score_sums((3,))
                        if scored and n == 6:
                            score_sums((2,))
                        if scored and n == 7:
                            score_sums((0, 1)).then_inc(hqk_sum, 1)
                        if st["N"] and n == 7:
                            dve.wait_ge(inv_psum, n_inv.up())
                            vec.tensor_tensor(attn_t[:, st["N"][1], :], acc_sb[:, :], misc[1][:, :],
                                              ALU.mult).then_inc(attn_ready, 1)
                        if g == 0 and ok(i + 1) and n in (8, 9):
                            dve.wait_ge(xt_hi_ready, n_xt.up())
                            vec.tensor_tensor(xt_lo[:, n - 8, :], misc[n - 8][:, :], f32(xt_hi[:, n - 8, :]),
                                              ALU.subtract).then_inc(xt_ready, 1)
                        if g == 1 and ok(i - 3) and n in (8, 9):
                            dve.wait_ge(x2t_hi_ready, n_x2t.up())
                            vec.tensor_tensor(x2t_lo[:, n - 8, :], misc[n - 8][:, :], f32(x2t_hi[:, n - 8, :]),
                                              ALU.subtract).then_inc(x2t_ready, 1)
                        if g == 2 and ok(i - 3) and n in (8, 9):
                            half = n - 8
                            if half == 0:
                                dve.wait_ge(yb_ready, n_yb.up())
                            dve.wait_ge(y_psum, n_y.up())
                            v = y_sb[:, 2 * half:2 * half + 2, :]
                            vec.tensor_tensor(v, v, misc[half][:, :].rearrange("p (t c) -> p t c", c=C),
                                              ALU.add).then_inc(y_ready, 1)
                        if scored and n == 9:
                            dve.wait_ge(h_masked, n_masked.now())
                            vec.tensor_reduce(head_max[:, :], head_probs[:, :, :], axis=AX_X,
                                              op=ALU.max).then_inc(h_max, 1)

            turn.batches(dve, body, N_BATCH)

        @block.gpsimd
        def _(pool):
            turn = Turn()
            n_own = turn.count(3 * 2 + NT)
            n_stats = [turn.count(1), turn.count(1), turn.count(1)]
            n_scaled = [turn.count(LN_PARTS) for _ in range(3)]
            n_x1n = turn.count(LN_PARTS)
            n_ctx = [turn.count(16) for _ in range(NT)]
            n_qk, n_sum, n_max = turn.count(NT), turn.count(NT), turn.count(NT)
            n_inv, n_pv, n_attended = turn.count(NT), turn.count(NT), turn.count(NT)
            n_x2, n_stored = turn.count(NT), turn.count(16)
            gp = nc.gpsimd

            def own(ins):
                ins.then_inc(pool_own, 1)
                pool.wait_ge(pool_own, n_own.up())

            gp.memset(ones[:, :], 1.0)
            gp.memset(ident[:, :], 0.0)
            gp.memset(mask_q[:, :], 0.0)
            gp.memset(mask_k[:, :], 0.0)
            gp.memset(head_mask[:, :, :], 0.0)
            gp.memset(minus_half[:, :], -0.5)
            gp.memset(minus_one[:, :], -1.0)
            gp.memset(eps[:, :], EPS)
            own(gp.memset(head_scores[:, :, :], 0.0))
            own(gp.memset(stack_k[STACK:STACK + 1, :, :, :].bitcast(F32), 1.0))
            own(gp.affine_select(out=ident[:, :], in_=ident[:, :], compare_op=ALU.not_equal, fill=1.0, base=0,
                                 pattern=[[-1, P]], channel_multiplier=1))
            gp.affine_select(out=mask_q[:, :], in_=mask_q[:, :], compare_op=ALU.is_ge, fill=MASKED, base=0,
                             pattern=[[-1, P]], channel_multiplier=1)
            gp.affine_select(out=mask_k[:, :], in_=mask_k[:, :], compare_op=ALU.is_ge, fill=MASKED, base=0,
                             pattern=[[1, P]], channel_multiplier=-1)
            gp.affine_select(out=head_mask[:, :, :], in_=head_mask[:, :, :], compare_op=ALU.is_ge, fill=MASKED,
                             base=0, pattern=[[1, NH], [-1, NH]], channel_multiplier=0)
            gp.tensor_copy(ident_b[:, :], ident[:, :])
            gp.tensor_copy(pick[:, 0:2], ident[:, 2 * D:P:D])
            gp.tensor_copy(pick[:, 2:4], ident[:, 0:2 * D:D]).then_inc(const_ready, 1)
            pool.wait_ge(const_ready, 1)

            def ln_coefficients(which):
                pool.wait_ge(ln_stats[which], n_stats[which].up())
                wait(pool, ln_done[which], n_scaled[which].up(LN_PARTS) - LN_PARTS)
                own(gp.tensor_tensor(ln_var[:, which, :], ln_mv[:, which, :, 1], eps[:, :], ALU.add))
                gp.tensor_tensor(ln_negm[:, which, :], ln_mv[:, which, :, 0], minus_one[:, :], ALU.mult)
                own(gp.tensor_tensor(ln_rstd[:, which, :], ln_var[:, which, :], minus_half[:, :], ALU.pow))
                gp.tensor_tensor(ln_bias[:, which, :], ln_negm[:, which, :], ln_rstd[:, which, :],
                                 ALU.mult).then_inc(ln_scale[which], 1)

            def body(i, b):
                for g in range(NG):
                    scored, attended, added = tiles(i, g)
                    if scored:
                        t = scored[1]
                        if t == 0:
                            pool.wait_ge(ln_done[1], n_x1n.up(LN_PARTS))
                        pool.wait_ge(ctx_loaded[t], n_ctx[t].up(16))
                        wait(pool, hqk_sum, n_qk.up() - 1)
                        for j in range(CHUNKS):
                            keys = 4 * (j + 1)
                            last = gp.tensor_tensor(
                                qk_prod[:, COFF[j]:COFF[j + 1]].rearrange("p (q k d) -> p q k d", q=4, d=HD),
                                x1n[:, t, 4 * j * HD:4 * (j + 1) * HD].rearrange("p (q o d) -> p q o d", o=1, d=HD)
                                .to_broadcast([P, 4, keys, HD]),
                                ctx_sb[:, t, 0:keys * HD].rearrange("p (o k d) -> p o k d", o=1, d=HD)
                                .to_broadcast([P, 4, keys, HD]), ALU.mult)
                        last.then_inc(hqk_prod, 1)
                    if g == 0 and ok(i + 1):
                        ln_coefficients(0)
                    if g == 1 and ok(i - 1):
                        ln_coefficients(1)
                    if attended:
                        t = attended[1]
                        pool.wait_ge(h_inv, n_inv.up())
                        own(gp.tensor_tensor(head_probs[:, :, :], head_probs[:, :, :],
                                             head_inv[:, :, None].to_broadcast([P, NH, NH]), ALU.mult))
                        wait(pool, hpv_sum, n_pv.up() - 1)
                        for j in range(CHUNKS):
                            keys = 4 * (j + 1)
                            last = gp.tensor_tensor(
                                pv_prod[:, COFF[j]:COFF[j + 1]].rearrange("p (q d k) -> p q d k", q=4, k=keys),
                                head_probs[:, 4 * j:4 * j + 4, None, 0:keys].to_broadcast([P, 4, HD, keys]),
                                ctx_sb[:, t, 0:keys * HD].rearrange("p (o k d) -> p o d k", o=1, d=HD)
                                .to_broadcast([P, 4, HD, keys]), ALU.mult)
                        last.then_inc(hpv_prod, 1)
                    if g == 3 and ok(i - 2):
                        ln_coefficients(2)
                        pool.wait_ge(x2_ready, n_x2.up(NT))
                        wait(pool, y_stored, n_stored.up(16) - 16)
                        gp.tensor_tensor(y_sb[:, :, :], x2[:, :, :],
                                         bias_bc[:, None, :].to_broadcast([P, NT, C]), ALU.add).then_inc(yb_ready, 1)
                    if scored:
                        pool.wait_ge(hqk_sum, n_sum.up())
                        wait(pool, hpv_prod, n_attended.up() - 1)
                        gp.tensor_tensor(head_probs[:, :, :], head_scores[:, :, :], head_mask[:, :, :],
                                         ALU.add).then_inc(h_masked, 1)
                        pool.wait_ge(h_max, n_max.up())
                        gp.tensor_tensor(head_probs[:, :, :], head_probs[:, :, :],
                                         head_max[:, :, None].to_broadcast([P, NH, NH]),
                                         ALU.subtract).then_inc(h_shifted, 1)

            pool.wait_ge(w_lo_ready, 1)
            pool.wait_ge(wf_ready, 1)
            pool.wait_ge(setup_act, 2)
            turn.batches(pool, body, N_BATCH)

    return nc


INPUTS = ["x", "ctx_1024", "L0_attn_Wq", "L0_attn_Wk", "L0_attn_Wv", "L0_attn_Wo",
          "L0_ffn_kernel", "L0_ffn_bias", "L0_ffn_a", "L0_ffn_b"]


def kernel(**inputs):
    import numpy as np
    import concourse.bacc as bacc
    from concourse.bass_utils import run_bass_kernel_spmd

    nc = bacc.Bacc("TRN2", target_bir_lowering=False, num_devices=1)
    arrays, args = {}, []
    for name in INPUTS:
        a = np.ascontiguousarray(inputs[name])
        arrays[f"in_{name}"] = a
        args.append(nc.dram_tensor(f"in_{name}", a.shape, mybir.dt.from_np(a.dtype), kind="ExternalInput").ap())
    shape = inputs["x"].shape
    result = nc.dram_tensor("out_0", shape, F32, kind="ExternalOutput").ap()
    decoder_layer(nc, *args, result)
    r = run_bass_kernel_spmd(nc, [arrays], core_ids=[0])
    return r.results[0]["out_0"]
```

```python
from contextlib import ExitStack

import concourse.bass as bass
from concourse import mybir

F32 = mybir.dt.float32
F32R = mybir.dt.float32r
BF16 = mybir.dt.bfloat16
ALU = mybir.AluOpType
ACT = mybir.ActivationFunctionType
AX_X = mybir.AxisListType.X

P = 128
MASKED = -1.0e30
EPS = 1e-5
QMAX = 7.0
ROUND = 1.5 * 2.0 ** 23


class Count:

    def __init__(self, turn, per_batch):
        self.turn, self.per_batch, self.total = turn, per_batch, 0

    def up(self, n=1):
        self.total += n
        return self.now()

    def now(self, back=0):
        value = self.total - back
        if self.turn.reg is None:
            return value
        assert value > 0
        return (self.turn.reg - self.turn.first) * self.per_batch + value


class Turn:

    def __init__(self):
        self.reg, self.first, self.counts = None, 0, []

    def count(self, per_batch):
        self.counts.append(Count(self, per_batch))
        return self.counts[-1]

    def batches(self, eng, body, n_batch):
        first, after = 3, n_batch - 2
        for i in range(-1, first):
            body(i, i)
        before = [c.total for c in self.counts]
        with eng.Fori(first, after) as reg:
            self.reg, self.first = reg, first
            body(first, reg)
        self.reg = None
        for c, was in zip(self.counts, before):
            assert c.total - was == c.per_batch, (c.total - was, c.per_batch)
            c.total += c.per_batch * (after - first - 1)
        for i in range(after, n_batch + 3):
            body(i, i)


def wait(eng, sem, value):
    if not isinstance(value, int) or value > 0:
        eng.wait_ge(sem, value)


def wait_apart(eng, long_past, *waits):
    for _, value in waits:
        if not isinstance(value, int):
            eng.compute_val(value)
    eng.wait_ge(long_past, 1)
    for sem, value in waits:
        wait(eng, sem, value)


def decoder_layer(nc, x, ctx_in, wq, wk, wv, wo, ffn_w, ffn_bias, ffn_a, ffn_b, out):
    N_BATCH, T, C = x.shape
    W = wq.shape[1]
    NH = 16
    D = W // NH
    HD = C // NH
    G = 4
    NG = NH // G
    NT = T // P
    CC = C // P
    RANK = ffn_a.shape[1]
    SLOTS = 4
    STACK = 3 * D
    SCALE = float(HD) ** -0.5
    assert D * G == P and D == 32 and NG == 4 and NT == 4 and CC == 2 and HD == 16 and T == 512
    UNITS = 10
    LN_PARTS = 2
    STACK_DMAS = 6
    PTR = 4
    CHUNKS = NH // 4
    COFF = [4 * 4 * HD * (j * (j + 1) // 2) for j in range(CHUNKS + 1)]

    x_t = x.rearrange("b (t p) c -> b p t c", p=P)
    ctx_t = ctx_in.rearrange("b (t p) c -> b p t c", p=P)
    out_t = out.rearrange("b (t p) c -> b p t c", p=P)

    def ok(b):
        return 0 <= b < N_BATCH

    with ExitStack() as ctx:
        def sb(name, shape, dt=F32):
            return ctx.enter_context(nc.sbuf_tensor(name, shape, dt))

        def psum(name, shape, dt=F32):
            return ctx.enter_context(nc.psum_tensor(name, shape, dt))

        def sem(name):
            return ctx.enter_context(nc.semaphore(name))

        stack_q = sb("stack_q", [P, SLOTS, G, T], F32R)
        stack_k = sb("stack_k", [P, SLOTS, G, T], F32R)
        q_hi = sb("q_hi", [P, T], F32R)
        q_lo = sb("q_lo", [P, T], F32R)
        k_hi = sb("k_hi", [P, T], F32R)
        k_lo = sb("k_lo", [P, T], F32R)
        values = sb("values", [P, SLOTS, NT, P])
        probs = sb("probs", [P, PTR, T])
        xt_hi = sb("xt_hi", [P, CC, T], F32R)
        xt_lo = sb("xt_lo", [P, CC, T], F32R)
        w_hi = sb("w_hi", [P, CC, 3 * W], F32R)
        w_lo = sb("w_lo", [P, CC, 3 * W], F32R)
        wo_sb = sb("wo_sb", [P, NG, C])
        seg_max = sb("seg_max", [P, G, NT])
        neg_max = sb("neg_max", [P, 2, G, NT])
        max_row = sb("max_row", [G * NT, 2, P], F32R)
        acc_sb = sb("acc_sb", [P, T])
        sum_sb = sb("sum_sb", [P, T])
        inv_sum = sb("inv_sum", [P, NT, G])
        attn_t = sb("attn_t", [P, NG, T])
        x_in = sb("x_in", [P, NT, C])
        x1 = sb("x1", [P, NT, C])
        x1n = sb("x1n", [P, NT, C])
        ctx_sb = sb("ctx_sb", [P, NT, C])
        x2 = sb("x2", [P, NT, C])
        x2n = sb("x2n", [P, NT, C])
        y_sb = sb("y_sb", [P, NT, C])
        x2t_hi = sb("x2t_hi", [P, CC, T], F32R)
        x2t_lo = sb("x2t_lo", [P, CC, T], F32R)
        wf_hi = sb("wf_hi", [P, CC, C], F32R)
        wf_lo = sb("wf_lo", [P, CC, C], F32R)
        prod = sb("prod", [P, 2, COFF[-1]])
        qk_prod, pv_prod = prod[:, 0, :], prod[:, 1, :]
        head_scores = sb("head_scores", [P, NH, NH])
        head_probs = sb("head_probs", [P, NH, NH])
        head_max = sb("head_max", [P, NH])
        head_sum = sb("head_sum", [P, NH])
        head_inv = sb("head_inv", [P, NH])
        head_out = sb("head_out", [P, C])
        ln_raw = sb("ln_raw", [P, 3, NT, 6])
        touched = sb("touched", [P, 3, 1])
        ln_mv = sb("ln_mv", [P, 3, NT, 2])
        ln_var = sb("ln_var", [P, 3, NT])
        ln_rstd = sb("ln_rstd", [P, 3, NT])
        ln_negm = sb("ln_negm", [P, 3, NT])
        ln_bias = sb("ln_bias", [P, 3, NT])
        ident = sb("ident", [P, P])
        ident_b = sb("ident_b", [P, P], BF16)
        mask_q = sb("mask_q", [P, P], BF16)
        mask_k = sb("mask_k", [P, P], BF16)
        ones = sb("ones", [P, P])
        minus_half, minus_one, eps = sb("minus_half", [P, NT]), sb("minus_one", [P, NT]), sb("eps", [P, NT])
        head_mask = sb("head_mask", [P, NH, NH], BF16)
        bias_bc = sb("bias_bc", [P, C])
        scal = sb("scal", [P, 8])
        late_scores = x_in[:, 0, :].rearrange("p (q k) -> p q k", k=NH)
        flat = prod[:, :, :].rearrange("p a n -> p (a n)")
        w_raw = flat[:, 0:CC * 3 * W].rearrange("p (c n) -> p c n", c=CC)
        fw_raw = flat[:, CC * 3 * W:CC * 3 * W + CC * C].rearrange("p (c n) -> p c n", c=CC)
        fw_q = flat[:, CC * 3 * W + CC * C:CC * 3 * W + 2 * CC * C].rearrange("p (c n) -> p c n", c=CC)
        a_raw = x2n[:, 0, 0:CC * RANK].rearrange("p (c r) -> p c r", c=CC)
        a_t = x2n[0:RANK, 1, 0:C]
        b_raw = x2n[0:RANK, 2, 0:C]
        bias_row = x2n[0:1, 3, 0:C]

        max_bank = [psum(f"max_bank{n}", [P, T]) for n in range(2)]
        exp_bank = [psum(f"exp_bank{n}", [P, T]) for n in range(2)]
        misc = [psum(f"misc{n}", [P, T]) for n in range(2)]
        acc_bank = psum("acc_bank", [P, T])
        sum_bank = psum("sum_bank", [P, T])

        w_loaded, wo_loaded, small_loaded = sem("w_loaded"), sem("wo_loaded"), sem("small_loaded")
        x_loaded, x1_loaded = sem("x_loaded"), sem("x1_loaded")
        ctx_loaded = [sem(f"ctx_loaded{t}") for t in range(NT)]
        const_ready, ones_ready = sem("const_ready"), sem("ones_ready")
        w_hi_ready, w_lo_ready = sem("w_hi_ready"), sem("w_lo_ready")
        wf_hi_ready, wf_ready = sem("wf_hi_ready"), sem("wf_ready")
        setup_pe, setup_dve, setup_act = sem("setup_pe"), sem("setup_dve"), sem("setup_act")
        ln_stats = [sem(f"ln{n}_stats") for n in range(3)]
        ln_scale = [sem(f"ln{n}_scale") for n in range(3)]
        ln_done = [sem(f"ln{n}_done") for n in range(3)]
        dve_own, pool_own = sem("dve_own"), sem("pool_own")
        xt_psum, xt_hi_ready, xt_ready = (sem("xt_psum"), sem("xt_hi_ready"), sem("xt_ready"))
        x2t_psum, x2t_hi_ready, x2t_ready = sem("x2t_psum"), sem("x2t_hi_ready"), sem("x2t_ready")
        qk_psum, qk_hi_ready, qk_lo_ready = sem("qk_psum"), sem("qk_hi_ready"), sem("qk_lo_ready")
        v_psum, v_ready = sem("v_psum"), sem("v_ready")
        stacked, max_stacked = sem("stacked"), sem("max_stacked")
        max_scored, max_taken, max_ready = sem("max_scored"), sem("max_taken"), sem("max_ready")
        max_psum, max_row_ready = sem("max_psum"), sem("max_row_ready")
        exp_scored, exp_done, pv_done = sem("exp_scored"), sem("exp_done"), sem("pv_done")
        acc_saved = sem("acc_saved")
        sums_psum, inv_ready, inv_psum, attn_ready = (sem("sums_psum"), sem("inv_ready"), sem("inv_psum"),
                                                      sem("attn_ready"))
        wo_psum = sem("wo_psum")
        y_psum, y_ready, y_stored = sem("y_psum"), sem("y_ready"), sem("y_stored")
        x1_added = sem("x1_added")
        hqk_prod, hqk_sum, h_masked, h_max, h_shifted = (sem("hqk_prod"), sem("hqk_sum"), sem("h_masked"),
                                                        sem("h_max"), sem("h_shifted"))
        h_exp, h_inv, hpv_prod, hpv_sum, h_out = (sem("h_exp"), sem("h_inv"), sem("hpv_prod"),
                                                  sem("hpv_sum"), sem("h_out"))
        hpv_first, sums_inverted = sem("hpv_first"), sem("sums_inverted")
        x2_ready, x1_kept, yb_ready = sem("x2_ready"), sem("x1_kept"), sem("yb_ready")

        block = ctx.enter_context(nc.Block())

        def key_units():
            for h in range(G):
                yield [(h, 0, 0, T)], (0, 1, 0)
            for h in range(G):
                yield [(h, 1, 0, 3 * P), (h, 3, 3 * P, P)], (0, 2, 3 * P)
            for h in range(0, G, 2):
                yield [(h, 2, 0, 2 * P), (h + 1, 2, 2 * P, 2 * P)], (0, 2, 2 * P)

        def query_units():
            for h in range(G):
                yield [(h, 3, 0, T)], (3 * P, 1, 0)
            for h in range(G):
                yield [(h, 2, 0, 3 * P), (h, 0, 3 * P, P)], (2 * P, 2, P)
            for h in range(0, G, 2):
                yield [(h, 1, 0, 2 * P), (h + 1, 1, 2 * P, 2 * P)], (P, 2, 2 * P)

        KEY_UNITS, QUERY_UNITS = list(key_units()), list(query_units())
        assert len(KEY_UNITS) == len(QUERY_UNITS) == UNITS

        def stages(i, g):
            def group(ahead):
                b, n = divmod(g + ahead, NG)
                return (b, n) if ok(i + b) else None
            return {"C": group(0), "B": group(2), "A": group(3), "M": group(1), "N": group(-1)}

        def values_pair(i, g):
            b, n = divmod(g + 2, NG)
            return (b, n // 2) if g % 2 == 0 and ok(i + b) else None

        def tiles(i, g):
            def tile(back):
                b, t = divmod(g - back, NT)
                return (b - 1, t) if ok(i + b - 1) else None
            return tile(2), tile(3), tile(4)

        LATE_VECTOR, LATE_POOL = (3, 0), (1, 2)
        FIRST_LATE = NG * N_BATCH - 2

        def late(i, g):
            return NG * i + g >= FIRST_LATE

        def was_late(i, g):
            return NG * i + g > FIRST_LATE

        def score_products(engine, t, chunks):
            for j in chunks:
                keys = 4 * (j + 1)
                last = engine.tensor_tensor(
                    qk_prod[:, COFF[j]:COFF[j + 1]].rearrange("p (q k d) -> p q k d", q=4, d=HD),
                    x1n[:, t, 4 * j * HD:4 * (j + 1) * HD].rearrange("p (q o d) -> p q o d", o=1, d=HD)
                    .to_broadcast([P, 4, keys, HD]),
                    ctx_sb[:, t, 0:keys * HD].rearrange("p (o k d) -> p o k d", o=1, d=HD)
                    .to_broadcast([P, 4, keys, HD]), ALU.mult)
            return last

        FFN_SETUP = (-1, 1)

        def by_head(w, c):
            return w[:, c, 0:2 * W].rearrange("p (n h d) -> p n d h", h=G, d=D)

        def by_row(w, c):
            return w[:, c, 0:2 * W].rearrange("p (n d h) -> p n d h", h=G, d=D)

        @block.sync
        def _(sp):
            turn = Turn()
            n_x_used = turn.count(CC)
            n_lo = turn.count(2 * NG)
            n_free = turn.count(UNITS * NG)
            n_row = turn.count(NG)
            n_kept = turn.count(1)
            n_pv = turn.count(NT)
            n_y, n_stored = turn.count(CC), turn.count(16)

            sp.dma_start(x_in[:, :, :], x_t[0]).then_inc(x_loaded, 16)
            for n, w in enumerate((wq, wk, wv)):
                sp.dma_start(w_raw[:, :, n * W:(n + 1) * W],
                             w.rearrange("(c p) n -> p c n", p=P)).then_inc(w_loaded, 16)
            sp.dma_start(wo_sb[:, :, :], wo.rearrange("(g p) n -> p g n", p=P)).then_inc(wo_loaded, 16)
            sp.dma_start(fw_raw, ffn_w.rearrange("(c p) n -> p c n", p=P)).then_inc(small_loaded, 16)
            sp.dma_start(a_raw, ffn_a.rearrange("(c p) r -> p c r", p=P)).then_inc(small_loaded, 16)
            sp.dma_start(b_raw, ffn_b).then_inc(small_loaded, 16)
            sp.dma_start(bias_row, ffn_bias.rearrange("(o n) -> o n", o=1)).then_inc(small_loaded, 16)

            def body(i, b):
                for g in range(NG):
                    st = stages(i, g)
                    if g == 1 and ok(i + 2):
                        wait_apart(sp, const_ready, (xt_psum, n_x_used.up(CC)))
                        sp.dma_start(x_in[:, :, :], x_t[b + 2]).then_inc(x_loaded, 16)
                    if g == 3 and ok(i - 3):
                        wait_apart(sp, const_ready, (y_ready, n_y.up(CC)))
                        sp.dma_start(out_t[b - 3], y_sb[:, :, :]).then_inc(y_stored, 16)
                        n_stored.up(16)
                    if ok(i - 1):
                        wait_apart(sp, const_ready, (hpv_prod, n_pv.up() - NT))
                        sp.dma_start(ctx_sb[:, g, :], ctx_t[b - 1, :, g, :]).then_inc(ctx_loaded[g], 16)
                    if st["A"]:
                        s = st["A"][1]
                        wait_apart(sp, const_ready, (qk_lo_ready, n_lo.up(2)),
                                   (exp_scored, n_free.up(UNITS) - UNITS * SLOTS))
                        for stack, parts in ((stack_q, (q_hi, q_lo, q_hi)), (stack_k, (k_hi, k_hi, k_lo))):
                            for n, part in enumerate(parts):
                                sp.dma_start(stack[n * D:(n + 1) * D, s, :, :].bitcast(F32),
                                             part[:, :].bitcast(F32)).then_inc(stacked, 16)
                    if st["M"]:
                        sp.wait_ge(max_row_ready, n_row.up())
                        m_slot = st["M"][1]
                        sp.dma_start(stack_q[STACK:STACK + 1, m_slot, :, :].bitcast(F32),
                                     max_row[:, m_slot % 2, :].bitcast(F32)).then_inc(max_stacked, 16)
                    if g == 0 and ok(i - 1):
                        if ok(i - 2):
                            wait_apart(sp, const_ready, (x1_kept, n_kept.up()))
                        sp.dma_start(x1[:, :, :], x_t[b - 1]).then_inc(x1_loaded, 16)

            turn.batches(sp, body, N_BATCH)
            sp.wait_ge(y_stored, n_stored.now())

        @block.tensor
        def _(pe):
            turn = Turn()
            n_ln = [turn.count(LN_PARTS), None, turn.count(LN_PARTS)]
            r_lo, r_v, r_row, r_xt = turn.count(2 * NG), turn.count(NG), turn.count(NG), turn.count(CC)
            r_inv, r_attn, r_x1 = turn.count(NG), turn.count(NG), turn.count(CC)
            r_x2t, r_y = turn.count(CC), turn.count(CC)
            readers = [[], []]
            n_xt, n_x2t = turn.count(CC), turn.count(CC)
            n_stack, n_row = turn.count(16 * STACK_DMAS * NG), turn.count(16 * NG)
            n_max_bank, n_max_ready = turn.count(UNITS * NG), turn.count(NG)
            n_exp_bank, n_probs, n_v = turn.count(UNITS * NG), turn.count(UNITS * NG), turn.count(NG)
            n_acc, n_sums, n_inv, n_attn = (turn.count(NG), turn.count(NG), turn.count(NG), turn.count(NG))

            def take(bank, reader, count):
                for s, c, total in readers[bank]:
                    wait(pe, s, c.now(c.total - total))
                count.up()
                readers[bank][:] = [(reader, count, count.total)]
                return misc[bank]

            def last_readers():
                readers[0][:] = [(v_ready, r_v, r_v.total)]
                readers[1][:] = [(attn_ready, r_attn, r_attn.total)]

            def mm(*args, **kw):
                return nc.tensor.matmul(*args, **kw)

            def split_terms(a_hi, a_lo, b_hi, b_lo):
                return ((a_hi, b_hi), (a_hi, b_lo), (a_lo, b_hi))

            def ffn_weights():
                pe.wait_ge(setup_dve, 1)
                nc.tensor.transpose(acc_bank[0:1, 0:P], scal[:, 0:1], ident[:, :]).then_inc(setup_pe, 1)
                pe.wait_ge(small_loaded, 64)
                for c in range(CC):
                    last = nc.tensor.transpose(sum_bank[0:RANK, c * P:(c + 1) * P], a_raw[:, c, :], ident[:, :])
                last.then_inc(setup_pe, 1)
                pe.wait_ge(setup_dve, 2)
                mm(acc_bank[:, 0:1], ones[0:1, 0:P], scal[0:1, 1:2], start=True, stop=True).then_inc(setup_pe, 1)
                pe.wait_ge(setup_act, 1)
                for c in range(CC):
                    last = mm(sum_bank[:, c * C:(c + 1) * C], a_t[:, c * P:(c + 1) * P], b_raw, start=True, stop=True)
                last.then_inc(setup_pe, 1)
                pe.wait_ge(setup_dve, 3)
                mm(acc_bank[:, 0:C], ones[0:1, 0:P], bias_row, start=True, stop=True).then_inc(setup_pe, 1)
                pe.wait_ge(setup_act, 2)
                pe.wait_ge(wf_ready, 1)
                pe.wait_ge(w_lo_ready, 2)
                pe.wait_ge(wo_loaded, 16)
                pe.wait_ge(ones_ready, 1)

            def transpose_tokens(src, sem_out, c, reader, count):
                bank = take(c, reader, count)
                for t in range(NT):
                    last = nc.tensor.transpose(bank[:, t * P:(t + 1) * P], src[:, t, c * P:(c + 1) * P], ident[:, :])
                last.then_inc(sem_out, 1)

            def project_qk(g, which):
                bank = take(which, qk_lo_ready, r_lo)
                n = 0
                for c in range(CC):
                    for wpart, xpart in split_terms(w_hi, w_lo, xt_hi, xt_lo):
                        last = mm(bank[:, :], wpart[:, c, which * W + g * P:which * W + (g + 1) * P],
                                  xpart[:, c, :], start=(n == 0), stop=(n == 5))
                        n += 1
                last.then_inc(qk_psum, 1)

            def project_v(pair, half):
                bank = take(1 - half, v_ready, r_v)
                for t in range(2):
                    tok = (2 * half + t) * P
                    n = 0
                    for c in range(CC):
                        for wpart, xpart in split_terms(w_hi, w_lo, xt_hi, xt_lo):
                            last = mm(bank[:, t * 2 * P:(t + 1) * 2 * P], xpart[:, c, tok:tok + P],
                                      wpart[:, c, 2 * W + pair * 2 * P:2 * W + (pair + 1) * 2 * P],
                                      start=(n == 0), stop=(n == 5))
                            n += 1
                last.then_inc(v_psum, 1)

            def scores(bank, unit, lhs, rhs, slot, rows, key_side, done):
                parts, (col, count, step) = unit
                for n, (h, blk, at, width) in enumerate(parts):
                    first = blk * P if key_side else 0
                    mm(bank[:, at:at + width], lhs[0:rows, slot, h, blk * P:(blk + 1) * P],
                       rhs[0:rows, slot, h, first:first + width], start=(n == 0), stop=False,
                       skip_group_check=True)
                mask = mask_k if key_side else mask_q
                if count == 1:
                    o, m = bank[:, col:col + P], mask[:, :]
                else:
                    o = bank[:, :].rearrange("p (a n) -> p a n", n=P)[:, col // P:col // P + step // P + 1:step // P, :]
                    m = mask[:, None, :].to_broadcast([P, 2, P])
                mm(o, ident_b[:, :], m, start=False, stop=True, skip_group_check=True).then_inc(done, 1)

            def attend(units, slot, first_tile):
                pe.wait_ge(exp_done, n_probs.up(len(units)))
                rounds = [[], []]
                for n in units:
                    for k, (h, blk, at, width) in enumerate(KEY_UNITS[n][0]):
                        p = probs[:, (first_tile + n) % PTR, at:at + width]
                        rounds[k if len(units) > 1 else 0].append((h, blk, T - width, p))
                for r in rounds:
                    for h, blk, q0, p in r:
                        mm(acc_bank[h * D:(h + 1) * D, q0:T], values[:, slot, blk, h * D:(h + 1) * D], p,
                           start=(blk == 0), stop=(blk == 2), skip_group_check=True)
                    for h, blk, q0, p in r:
                        hs = (h + 2) % G
                        last = mm(sum_bank[hs * D:(hs + 1) * D, q0:T], ones[:, 0:D], p,
                                  start=(blk == 0), stop=(blk == 2), skip_group_check=True)
                last.then_inc(pv_done, len(units))

            def output_projection(half):
                bank = take(half, x1_added, r_x1)
                for t in range(2):
                    for k in range(NG):
                        last = mm(bank[:, t * C:(t + 1) * C],
                                  attn_t[:, k, (2 * half + t) * P:(2 * half + t + 1) * P],
                                  wo_sb[:, k, :], start=(k == 0), stop=(k == NG - 1))
                last.then_inc(wo_psum, 1)

            def ffn(half):
                bank = take(half, y_ready, r_y)
                for t in range(2):
                    tok = (2 * half + t) * P
                    k = 0
                    for c in range(CC):
                        for xpart, wpart in split_terms(x2t_hi, x2t_lo, wf_hi, wf_lo):
                            last = mm(bank[:, t * C:(t + 1) * C], xpart[:, c, tok:tok + P],
                                      wpart[:, c, :], start=(k == 0), stop=(k == 5))
                            k += 1
                last.then_inc(y_psum, 1)

            def body(i, b):
                if 1 <= i < N_BATCH:
                    last_readers()
                for g in range(NG):
                    st = stages(i, g)
                    first_tile = UNITS * g
                    if (i, g) == FFN_SETUP:
                        pe.wait_ge(w_lo_ready, 1)
                    if st["C"]:
                        pe.wait_ge(max_stacked, n_row.up(16))
                    if st["B"]:
                        pe.wait_ge(stacked, n_stack.up(16 * STACK_DMAS))
                    for n in range(UNITS):
                        if st["C"]:
                            wait(pe, exp_done, n_exp_bank.up() - 2)
                            scores(exp_bank[n % 2], KEY_UNITS[n], stack_k, stack_q, st["C"][1], STACK + 1,
                                   True, exp_scored)
                        if st["B"]:
                            wait(pe, max_taken, n_max_bank.up() - 2)
                            scores(max_bank[n % 2], QUERY_UNITS[n], stack_q, stack_k, st["B"][1], STACK,
                                   False, max_scored)
                        if st["N"] and n == 0:
                            attend((8, 9), st["N"][1], first_tile - UNITS)
                        if st["C"]:
                            if n == 2:
                                if g % 2 == 0:
                                    pe.wait_ge(v_ready, n_v.up(2))
                                wait(pe, acc_saved, n_acc.up() - 1)
                            if n in (2, 4, 6, 8):
                                attend((n - 2, n - 1), st["C"][1], first_tile)
                        if g == 1 and ok(i - 1) and n == 0:
                            output_projection(1)
                        if st["A"] and n in (1, 2):
                            if n == 1 and st["A"][1] == 0:
                                pe.wait_ge(xt_ready, n_xt.up(CC))
                            project_qk(st["A"][1], n - 1)
                        if st["N"] and n == 3:
                            pe.wait_ge(acc_saved, n_sums.up())
                            bank = take(0, inv_ready, r_inv)
                            for t in range(NT):
                                last = nc.tensor.transpose(bank[:, t * P:(t + 1) * P],
                                                           sum_sb[:, t * P:(t + 1) * P], ident[:, :])
                            last.then_inc(sums_psum, 1)
                        if st["M"] and n == 4:
                            pe.wait_ge(max_ready, n_max_ready.up())
                            bank = take(1, max_row_ready, r_row)
                            nc.tensor.transpose(bank[0:G * NT, 0:P],
                                                neg_max[:, st["M"][1] % 2, :, :].rearrange("p h t -> p (h t)"),
                                                ident[:, :]).then_inc(max_psum, 1)
                        if values_pair(i, g) and n in (0, 5):
                            project_v(values_pair(i, g)[1], n // 5)
                        if st["N"] and n == 6:
                            pe.wait_ge(inv_ready, n_inv.up())
                            bank = take(1, attn_ready, r_attn)
                            for t in range(NT):
                                last = nc.tensor.transpose(
                                    bank[:, t * P:(t + 1) * P],
                                    sum_sb[:, t * P:(t + 1) * P], ident[:, :])
                            last.then_inc(inv_psum, 1)
                        if g == 0 and ok(i + 1) and n in (7, 8):
                            if n == 7:
                                pe.wait_ge(ln_done[0], n_ln[0].up(LN_PARTS))
                            transpose_tokens(x_in, xt_psum, n - 7, xt_ready, r_xt)
                        if g == 0 and ok(i - 1) and n == 9:
                            pe.wait_ge(attn_ready, n_attn.up(NG))
                            output_projection(0)
                        if g == 1 and ok(i - 3) and n in (7, 8):
                            if n == 7:
                                pe.wait_ge(ln_done[2], n_ln[2].up(LN_PARTS))
                            transpose_tokens(x2n, x2t_psum, n - 7, x2t_ready, r_x2t)
                        if g == 2 and ok(i - 3) and n in (7, 8):
                            if n == 7:
                                pe.wait_ge(x2t_ready, n_x2t.up(CC))
                            ffn(n - 7)
                    if (i, g) == FFN_SETUP:
                        ffn_weights()

            pe.wait_ge(const_ready, 1)
            turn.batches(pe, body, N_BATCH)

        @block.scalar
        def _(act):
            turn = Turn()
            n_ln = [turn.count(1), turn.count(1), turn.count(1)]
            n_ln2, n_inverted = turn.count(LN_PARTS), turn.count(NG)
            n_xt, n_x2t, n_yb = turn.count(CC), turn.count(CC), turn.count(1)
            n_qk, n_staged = turn.count(2 * NG), turn.count(16 * STACK_DMAS * NG)
            n_v, n_values = turn.count(NG), turn.count(UNITS * NG)
            n_row, n_row_free = turn.count(NG), turn.count(16 * NG)
            n_exp, n_saved, n_norm = turn.count(UNITS * NG), turn.count(UNITS * NG), turn.count(NG)
            n_x1n, n_shift = turn.count(NT), turn.count(NT)

            def copy(dst, src):
                return nc.scalar.activation(dst, src, ACT.Identity)

            def layernorm(which, src, dst, part):
                if part == 0:
                    act.wait_ge(ln_scale[which], n_ln[which].up())
                for t in (2 * part, 2 * part + 1):
                    last = nc.scalar.activation(dst[:, t, :], src[:, t, :], ACT.Identity,
                                                bias=ln_bias[:, which, t:t + 1], scale=ln_rstd[:, which, t:t + 1])
                last.then_inc(ln_done[which], 1)

            layernorm(0, x_in, x_in, 0)
            layernorm(0, x_in, x_in, 1)
            act.wait_ge(w_loaded, 48)
            for c in range(CC):
                last = copy(by_row(w_hi, c), by_head(w_raw, c))
            last.then_inc(w_hi_ready, 1)

            def ffn_weights():
                copy(w_hi[:, :, 2 * W:], w_raw[:, :, 2 * W:]).then_inc(w_hi_ready, 1)
                act.wait_ge(setup_pe, 2)
                copy(a_t, sum_bank[0:RANK, 0:C]).then_inc(setup_act, 1)
                act.wait_ge(setup_pe, 5)
                copy(bias_bc[:, :], acc_bank[:, 0:C]).then_inc(setup_act, 1)

            def body(i, b):
                for g in range(NG):
                    st = stages(i, g)
                    scored, attended, added = tiles(i, g)
                    for n in range(UNITS):
                        if st["C"]:
                            act.wait_ge(exp_scored, n_exp.up())
                            wait(act, pv_done, n_exp.now(PTR) if turn.reg is not None or n_exp.total > PTR else 0)
                            nc.scalar.activation(probs[:, (UNITS * g + n) % PTR, :], exp_bank[n % 2][:, :],
                                                 ACT.Exp, scale=SCALE).then_inc(exp_done, 1)
                        if attended and n == (0 if late(i, g) else 1):
                            act.wait_ge(h_shifted, n_shift.up())
                            if was_late(i, g):
                                act.wait_ge(hpv_prod, n_shift.now(1))
                            src = late_scores if was_late(i, g) else head_probs[:, :, :]
                            nc.scalar.activation(head_probs[:, :, :], src, ACT.Exp,
                                                 scale=SCALE).then_inc(h_exp, 1)
                        if st["N"] and n == 1:
                            act.wait_ge(pv_done, n_saved.up(UNITS))
                            wait(act, attn_ready, n_norm.up() - 1)
                            copy(acc_sb[:, :], acc_bank[:, :])
                            copy(sum_sb[:, :], sum_bank[:, :]).then_inc(acc_saved, 1)
                        if st["A"] and n in (1, 2):
                            act.wait_ge(qk_psum, n_qk.up())
                            if n == 1:
                                wait(act, stacked, n_staged.up(16 * STACK_DMAS) - 16 * STACK_DMAS)
                            copy((q_hi, k_hi)[n - 1][:, :], misc[n - 1][:, :]).then_inc(qk_hi_ready, 1)
                        if g == 0 and ok(i - 3) and n in (2, 3):
                            layernorm(2, x2, x2n, n - 2)
                        if st["N"] and n == 4:
                            act.wait_ge(sums_inverted, n_inverted.up())
                            copy(sum_sb[:, :].rearrange("p (a d) -> p a d", d=D),
                                 inv_sum[:, :, :].rearrange("p t h -> p (t h)")[:, :, None]
                                 .to_broadcast([P, NT * G, D])).then_inc(inv_ready, 1)
                        if st["M"] and n == 5:
                            act.wait_ge(max_psum, n_row.up())
                            wait(act, max_stacked, n_row_free.up(16) - 32)
                            copy(max_row[:, st["M"][1] % 2, :], misc[1][0:G * NT, 0:P]).then_inc(max_row_ready, 1)
                        if values_pair(i, g) and n in (1, 5):
                            act.wait_ge(v_psum, n_v.up())
                            if n == 1:
                                wait(act, pv_done, n_values.up(2 * UNITS) - UNITS * SLOTS)
                            slot, half = 2 * values_pair(i, g)[1], n // 5
                            copy(values[:, slot:slot + 2, 2 * half:2 * half + 2, :],
                                 misc[1 - half][:, :].rearrange("p (t s n) -> p s t n", t=2, s=2)).then_inc(v_ready, 1)
                        if g == 3 and ok(i + 2) and n in (5, 6):
                            layernorm(0, x_in, x_in, n - 5)
                        if g == 1 and ok(i - 1) and n in (5, 6):
                            if n == 5:
                                wait(act, hqk_prod, n_x1n.up(NT) - NT)
                            layernorm(1, x1, x1n, n - 5)
                        if g == 0 and ok(i + 1) and n in (7, 8):
                            act.wait_ge(xt_psum, n_xt.up())
                            copy(xt_hi[:, n - 7, :], misc[n - 7][:, :]).then_inc(xt_hi_ready, 1)
                        if g == 1 and ok(i - 3) and n in (7, 8):
                            act.wait_ge(x2t_psum, n_x2t.up())
                            copy(x2t_hi[:, n - 7, :], misc[n - 7][:, :]).then_inc(x2t_hi_ready, 1)
                        if g == 0 and ok(i - 2) and n == 4:
                            wait(act, yb_ready, n_yb.up() - 1)
                            wait(act, ln_done[2], n_ln2.up(LN_PARTS) - LN_PARTS)
                            copy(x2[:, :, :], x1[:, :, :]).then_inc(x1_kept, 1)
                    if (i, g) == FFN_SETUP:
                        ffn_weights()

            turn.batches(act, body, N_BATCH)

        @block.vector
        def _(dve):
            turn = Turn()
            n_own = turn.count(3 + NT)
            n_x, n_x1 = turn.count(16), turn.count(16)
            n_scale = [turn.count(1), turn.count(1), turn.count(1)]
            n_hi, n_xt, n_x2t = turn.count(2 * NG), turn.count(CC), turn.count(CC)
            n_scored, n_row = turn.count(UNITS * NG), turn.count(NG)
            n_sums, n_inv = turn.count(NG), turn.count(NG)
            n_wo, n_y, n_yb = turn.count(CC), turn.count(CC), turn.count(1)
            n_prod, n_masked, n_exp = turn.count(NT), turn.count(NT), turn.count(NT)
            n_pv, n_kept, n_norm = turn.count(NT), turn.count(1), turn.count(NT)

            def own(ins):
                ins.then_inc(dve_own, 1)
                dve.wait_ge(dve_own, n_own.up())

            def f32(ap):
                return ap.bitcast(F32)

            vec = nc.vector

            def ffn_weights():
                dve.wait_ge(w_hi_ready, 2)
                vec.tensor_tensor(w_lo[:, :, 2 * W:], w_raw[:, :, 2 * W:], f32(w_hi[:, :, 2 * W:]),
                                  ALU.subtract).then_inc(w_lo_ready, 1)
                dve.wait_ge(small_loaded, 64)
                fw_flat = fw_raw.rearrange("p c n -> p (c n)")
                vec.tensor_reduce(scal[:, 0:1], fw_flat, axis=AX_X, op=ALU.max,
                                  apply_absolute_value=True).then_inc(setup_dve, 1)
                dve.wait_ge(setup_pe, 1)
                vec.tensor_reduce(scal[0:1, 1:2], acc_bank[0:1, 0:P], axis=AX_X, op=ALU.max).then_inc(setup_dve, 1)
                dve.wait_ge(setup_pe, 3)
                own(vec.tensor_scalar(scal[:, 2:3], acc_bank[:, 0:1], 1.0 / QMAX, None, ALU.mult))
                vec.reciprocal(scal[:, 3:4], scal[:, 2:3]).then_inc(setup_dve, 1)
                dve.wait_ge(setup_dve, 3)
                own(vec.tensor_scalar(fw_q, fw_raw, scal[:, 3:4], None, ALU.mult))
                own(vec.tensor_scalar(fw_q, fw_q, ROUND, None, ALU.add))
                own(vec.tensor_scalar(fw_q, fw_q, -ROUND, None, ALU.add))
                own(vec.tensor_scalar(fw_q, fw_q, -QMAX - 1.0, QMAX, ALU.max, ALU.min))
                own(vec.tensor_scalar(fw_q, fw_q, scal[:, 2:3], None, ALU.mult))
                dve.wait_ge(setup_pe, 4)
                own(vec.tensor_tensor(fw_q, fw_q, sum_bank[:, :].rearrange("p (c n) -> p c n", c=CC), ALU.add))
                vec.tensor_copy(wf_hi[:, :, :], fw_q).then_inc(wf_hi_ready, 1)
                dve.wait_ge(wf_hi_ready, 1)
                vec.tensor_tensor(wf_lo[:, :, :], fw_q, f32(wf_hi[:, :, :]), ALU.subtract).then_inc(wf_ready, 1)

            def ln_statistics(which, src, part):
                if part == 0:
                    wait(dve, ln_scale[which], n_scale[which].up() - 1)
                for t in (2 * part, 2 * part + 1):
                    last = vec.bn_stats(ln_raw[:, which, t, :], src[:, t, :])
                if part == 0:
                    return
                last.then_inc(dve_own, 1)
                dve.wait_ge(dve_own, n_own.up())
                vec.tensor_copy(touched[:, which, :], ln_raw[:, which, 0, 0:1])
                for t in range(NT):
                    last = vec.bn_aggr(ln_mv[:, which, t, :], ln_raw[:, which, t, :])
                last.then_inc(ln_stats[which], 1)

            def take_max(n, ring):
                dve.wait_ge(max_scored, n_scored.up())
                bank = max_bank[n % 2]
                if n < G:
                    o, v = neg_max[:, ring, n:n + 1, 3], bank[:, :]
                elif n < 2 * G:
                    o, v = seg_max[:, n - G, :], bank[:, :].rearrange("p (s k) -> p s k", k=P)
                else:
                    h = 2 * (n - 2 * G)
                    o, v = neg_max[:, ring, h:h + 2, 1], bank[:, :].rearrange("p (s k) -> p s k", k=2 * P)
                vec.tensor_reduce(o, v, axis=AX_X, op=ALU.max, negate=True).then_inc(max_taken, 1)

            def sum_products(out, products, chunks):
                for j in chunks:
                    last = vec.tensor_reduce(out(j), products(j), axis=AX_X, op=ALU.add)
                return last

            def score_sums(chunks):
                return sum_products(
                    lambda j: head_scores[:, 4 * j:4 * j + 4, 0:4 * (j + 1)],
                    lambda j: qk_prod[:, COFF[j]:COFF[j + 1]].rearrange("p (q k d) -> p q k d", q=4, d=HD), chunks)

            def value_sums(chunks):
                return sum_products(
                    lambda j: head_out[:, j * 4 * HD:(j + 1) * 4 * HD],
                    lambda j: pv_prod[:, COFF[j]:COFF[j + 1]].rearrange("p (a k) -> p a k", k=4 * (j + 1)), chunks)

            def tile_inverses(i, g):
                dve.wait_ge(h_exp, n_exp.up())
                own(vec.tensor_reduce(head_sum[:, :], head_probs[:, :, :], axis=AX_X, op=ALU.add))
                wait(dve, hpv_prod, n_norm.up() - 1)
                last = vec.reciprocal(head_inv[:, :], head_sum[:, :])
                if late(i, g):
                    own(last)
                    last = vec.tensor_tensor(head_probs[:, :, :], head_probs[:, :, :],
                                             head_inv[:, :, None].to_broadcast([P, NH, NH]), ALU.mult)
                last.then_inc(h_inv, 1)

            def add_to_x1(half):
                dve.wait_ge(wo_psum, n_wo.up())
                v = x1[:, 2 * half:2 * half + 2, :]
                vec.tensor_tensor(v, v, misc[half][:, :].rearrange("p (t c) -> p t c", c=C),
                                  ALU.add).then_inc(x1_added, 1)

            def body(i, b):
                for g in range(NG):
                    st = stages(i, g)
                    scored, attended, added = tiles(i, g)
                    for n in range(UNITS):
                        if st["B"]:
                            ring = st["B"][1] % 2
                            if n == 0:
                                wait(dve, max_psum, n_row.up() - 2)
                            take_max(n, ring)
                            if n == UNITS - 1:
                                dve.wait_ge(max_taken, n_scored.now())
                                vec.tensor_reduce(neg_max[:, ring, :, 2], seg_max[:, :, 0:3], axis=AX_X, op=ALU.min)
                                vec.tensor_copy(neg_max[:, ring, :, 0], seg_max[:, :, 3]).then_inc(max_ready, 1)
                        if g == 1 and ok(i - 1) and n == 0:
                            dve.wait_ge(x1_loaded, n_x1.up(16))
                            add_to_x1(0)
                        if st["A"] and n in (2, 3):
                            dve.wait_ge(qk_hi_ready, n_hi.up())
                            which = int(n == 3)
                            hi, lo = ((q_hi, q_lo), (k_hi, k_lo))[which]
                            vec.tensor_tensor(lo[:, :], misc[which][:, :], f32(hi[:, :]),
                                              ALU.subtract).then_inc(qk_lo_ready, 1)
                        if scored and late(i, g) and n == 0:
                            t = scored[1]
                            dve.wait_ge(ctx_loaded[t], 16 * (b + scored[0] + 1))
                            dve.wait_ge(ln_done[1], LN_PARTS * (b + scored[0] + 1))
                            dve.wait_ge(hqk_sum, n_prod.now())
                            own(score_products(vec, t, LATE_VECTOR))
                        if g == 3 and ok(i - 2) and n in (7, 8):
                            dve.wait_ge(x2_ready, n_pv.now())
                            ln_statistics(2, x2, n - 7)
                        if attended and late(i, g) and n == 0:
                            tile_inverses(i, g)
                        if added and n == 0:
                            dve.wait_ge(hpv_prod, n_pv.up())
                            wait(dve, x2_ready, n_pv.now(1))
                            value_sums((0, 1)).then_inc(hpv_first, 1)
                            value_sums((2, 3)).then_inc(hpv_sum, 1)
                        if g == 2 and ok(i + 2) and n in (2, 4):
                            if n == 2:
                                dve.wait_ge(x_loaded, n_x.up(16))
                            ln_statistics(0, x_in, int(n == 4))
                        if g == 1 and ok(i - 1) and n == 1:
                            add_to_x1(1)
                        if g == 1 and ok(i - 1) and n in (1, 2):
                            dve.wait_ge(x1_added, n_wo.now(2 - n))
                            ln_statistics(1, x1, n - 1)
                        if st["N"] and n == 3:
                            dve.wait_ge(sums_psum, n_sums.up())
                            wait(dve, inv_ready, n_sums.now(1))
                            sums = misc[0][:, :].rearrange("p (t h d) -> p t h d", h=G, d=D)
                            vec.reciprocal(inv_sum[:, :, 0:2], sums[:, :, 2:4, 0])
                            vec.reciprocal(inv_sum[:, :, 2:4], sums[:, :, 0:2, 0]).then_inc(sums_inverted, 1)
                        if attended and not late(i, g) and n == 2:
                            tile_inverses(i, g)
                        if added and n == 4:
                            t = added[1]
                            if t == 0:
                                dve.wait_ge(x1_kept, n_kept.up())
                            dve.wait_ge(hpv_sum, n_pv.now())
                            vec.tensor_tensor(x2[:, t, :], x2[:, t, :], head_out[:, :], ALU.add).then_inc(x2_ready, 1)
                        if st["N"] and n == 7:
                            dve.wait_ge(inv_psum, n_inv.up())
                            vec.tensor_tensor(attn_t[:, st["N"][1], :], acc_sb[:, :], misc[1][:, :],
                                              ALU.mult).then_inc(attn_ready, 1)
                        if scored and n == 5:
                            dve.wait_ge(hqk_prod, n_prod.up())
                            wait(dve, h_masked, n_masked.up() - 1)
                            score_sums((3, 2))
                        if scored and n == 8:
                            score_sums((0, 1)).then_inc(hqk_sum, 1)
                        if g == 0 and ok(i + 1) and n in (8, 9):
                            dve.wait_ge(xt_hi_ready, n_xt.up())
                            vec.tensor_tensor(xt_lo[:, n - 8, :], misc[n - 8][:, :], f32(xt_hi[:, n - 8, :]),
                                              ALU.subtract).then_inc(xt_ready, 1)
                        if g == 1 and ok(i - 3) and n in (8, 9):
                            dve.wait_ge(x2t_hi_ready, n_x2t.up())
                            vec.tensor_tensor(x2t_lo[:, n - 8, :], misc[n - 8][:, :], f32(x2t_hi[:, n - 8, :]),
                                              ALU.subtract).then_inc(x2t_ready, 1)
                        if g == 2 and ok(i - 3) and n in (8, 9):
                            half = n - 8
                            if half == 0:
                                dve.wait_ge(yb_ready, n_yb.up())
                            dve.wait_ge(y_psum, n_y.up())
                            v = y_sb[:, 2 * half:2 * half + 2, :]
                            vec.tensor_tensor(v, v, misc[half][:, :].rearrange("p (t c) -> p t c", c=C),
                                              ALU.add).then_inc(y_ready, 1)
                        if scored and n == 9:
                            masked = head_probs[:, :, :]
                            if late(i, g):
                                masked = late_scores
                                dve.wait_ge(hqk_sum, n_prod.now())
                                dve.wait_ge(h_exp, n_exp.now())
                                vec.tensor_tensor(masked, head_scores[:, :, :], head_mask[:, :, :],
                                                  ALU.add).then_inc(h_masked, 1)
                            dve.wait_ge(h_masked, n_masked.now())
                            vec.tensor_reduce(head_max[:, :], masked, axis=AX_X, op=ALU.max).then_inc(h_max, 1)
                            if late(i, g):
                                dve.wait_ge(h_max, n_masked.now())
                                vec.tensor_tensor(masked, masked, head_max[:, :, None].to_broadcast([P, NH, NH]),
                                                  ALU.subtract).then_inc(h_shifted, 1)
                    if (i, g) == FFN_SETUP:
                        ffn_weights()

            dve.wait_ge(x_loaded, n_x.up(16))
            ln_statistics(0, x_in, 0)
            ln_statistics(0, x_in, 1)
            dve.wait_ge(w_hi_ready, 1)
            for c in range(CC):
                last = vec.tensor_tensor(by_row(w_lo, c), by_head(w_raw, c), f32(by_row(w_hi, c)), ALU.subtract)
            last.then_inc(w_lo_ready, 1)
            turn.batches(dve, body, N_BATCH)

        @block.gpsimd
        def _(pool):
            turn = Turn()
            n_own = turn.count(3 * 2 + NT)
            n_stats = [turn.count(1), turn.count(1), turn.count(1)]
            n_scaled = [turn.count(LN_PARTS) for _ in range(3)]
            n_x1n = turn.count(LN_PARTS)
            n_ctx = [turn.count(16) for _ in range(NT)]
            n_qk, n_sum, n_max = turn.count(NT), turn.count(NT), turn.count(NT)
            n_inv, n_pv, n_attended = turn.count(NT), turn.count(NT), turn.count(NT)
            n_x2, n_stored = turn.count(NT), turn.count(16)
            gp = nc.gpsimd

            def own(ins):
                ins.then_inc(pool_own, 1)
                pool.wait_ge(pool_own, n_own.up())

            def ln_coefficients(which):
                pool.wait_ge(ln_stats[which], n_stats[which].up())
                wait(pool, ln_done[which], n_scaled[which].up(LN_PARTS) - LN_PARTS)
                own(gp.tensor_tensor(ln_var[:, which, :], ln_mv[:, which, :, 1], eps[:, :], ALU.add))
                gp.tensor_tensor(ln_negm[:, which, :], ln_mv[:, which, :, 0], minus_one[:, :], ALU.mult)
                own(gp.tensor_tensor(ln_rstd[:, which, :], ln_var[:, which, :], minus_half[:, :], ALU.pow))
                gp.tensor_tensor(ln_bias[:, which, :], ln_negm[:, which, :], ln_rstd[:, which, :],
                                 ALU.mult).then_inc(ln_scale[which], 1)

            gp.memset(ones[:, :], 1.0)
            gp.memset(ident[:, :], 0.0)
            gp.memset(mask_q[:, :], 0.0)
            gp.memset(mask_k[:, :], 0.0)
            gp.memset(head_mask[:, :, :], 0.0)
            gp.memset(minus_half[:, :], -0.5)
            gp.memset(minus_one[:, :], -1.0)
            gp.memset(eps[:, :], EPS)
            own(gp.memset(head_scores[:, :, :], 0.0))
            ln_coefficients(0)
            own(gp.affine_select(out=ident[:, :], in_=ident[:, :], compare_op=ALU.not_equal, fill=1.0, base=0,
                                 pattern=[[-1, P]], channel_multiplier=1))
            gp.affine_select(out=mask_q[:, :], in_=mask_q[:, :], compare_op=ALU.is_ge, fill=MASKED, base=0,
                             pattern=[[-1, P]], channel_multiplier=1)
            gp.affine_select(out=mask_k[:, :], in_=mask_k[:, :], compare_op=ALU.is_ge, fill=MASKED, base=0,
                             pattern=[[1, P]], channel_multiplier=-1)
            gp.affine_select(out=head_mask[:, :, :], in_=head_mask[:, :, :], compare_op=ALU.is_ge, fill=MASKED,
                             base=0, pattern=[[1, NH], [-1, NH]], channel_multiplier=0)
            gp.tensor_copy(ident_b[:, :], ident[:, :]).then_inc(const_ready, 1)
            pool.wait_ge(const_ready, 1)
            gp.memset(stack_k[STACK:STACK + 1, :, :, :].bitcast(F32), 1.0).then_inc(ones_ready, 1)
            pool.wait_ge(ones_ready, 1)

            def body(i, b):
                for g in range(NG):
                    scored, attended, added = tiles(i, g)
                    if scored:
                        t = scored[1]
                        if t == 0:
                            pool.wait_ge(ln_done[1], n_x1n.up(LN_PARTS))
                            if i == 1:
                                pool.wait_ge(w_lo_ready, 2)
                                pool.wait_ge(wf_ready, 1)
                                pool.wait_ge(setup_act, 2)
                        pool.wait_ge(ctx_loaded[t], n_ctx[t].up(16))
                        wait(pool, hqk_sum, n_qk.up() - 1)
                        score_products(gp, t, LATE_POOL if late(i, g) else range(CHUNKS)).then_inc(hqk_prod, 1)
                    if g == 3 and ok(i + 2):
                        ln_coefficients(0)
                    if g == 1 and ok(i - 1):
                        ln_coefficients(1)
                    if attended:
                        t = attended[1]
                        pool.wait_ge(h_inv, n_inv.up())
                        if not late(i, g):
                            own(gp.tensor_tensor(head_probs[:, :, :], head_probs[:, :, :],
                                                 head_inv[:, :, None].to_broadcast([P, NH, NH]), ALU.mult))
                        wait(pool, hpv_first, n_pv.up() - 1)
                        for j in range(CHUNKS):
                            if j == 2:
                                wait(pool, hpv_sum, n_pv.now(1))
                            keys = 4 * (j + 1)
                            last = gp.tensor_tensor(
                                pv_prod[:, COFF[j]:COFF[j + 1]].rearrange("p (q d k) -> p q d k", q=4, k=keys),
                                head_probs[:, 4 * j:4 * j + 4, None, 0:keys].to_broadcast([P, 4, HD, keys]),
                                ctx_sb[:, t, 0:keys * HD].rearrange("p (o k d) -> p o d k", o=1, d=HD)
                                .to_broadcast([P, 4, HD, keys]), ALU.mult)
                        last.then_inc(hpv_prod, 1)
                    if scored and not late(i, g):
                        pool.wait_ge(hqk_sum, n_sum.up())
                        wait(pool, hpv_prod, n_attended.up() - 1)
                        gp.tensor_tensor(head_probs[:, :, :], head_scores[:, :, :], head_mask[:, :, :],
                                         ALU.add).then_inc(h_masked, 1)
                        pool.wait_ge(h_max, n_max.up())
                        gp.tensor_tensor(head_probs[:, :, :], head_probs[:, :, :],
                                         head_max[:, :, None].to_broadcast([P, NH, NH]),
                                         ALU.subtract).then_inc(h_shifted, 1)
                    if g == 3 and ok(i - 2):
                        ln_coefficients(2)
                        pool.wait_ge(x2_ready, n_x2.up(NT))
                        wait(pool, y_stored, n_stored.up(16) - 16)
                        gp.tensor_tensor(y_sb[:, :, :], x2[:, :, :],
                                         bias_bc[:, None, :].to_broadcast([P, NT, C]), ALU.add).then_inc(yb_ready, 1)

            turn.batches(pool, body, N_BATCH)

    return nc


INPUTS = ["x", "ctx_1024", "L0_attn_Wq", "L0_attn_Wk", "L0_attn_Wv", "L0_attn_Wo",
          "L0_ffn_kernel", "L0_ffn_bias", "L0_ffn_a", "L0_ffn_b"]


def kernel(**inputs):
    import numpy as np
    import concourse.bacc as bacc
    from concourse.bass_utils import run_bass_kernel_spmd

    nc = bacc.Bacc("TRN2", target_bir_lowering=False, num_devices=1)
    arrays, args = {}, []
    for name in INPUTS:
        a = np.ascontiguousarray(inputs[name])
        arrays[f"in_{name}"] = a
        args.append(nc.dram_tensor(f"in_{name}", a.shape, mybir.dt.from_np(a.dtype), kind="ExternalInput").ap())
    shape = inputs["x"].shape
    result = nc.dram_tensor("out_0", shape, F32, kind="ExternalOutput").ap()
    decoder_layer(nc, *args, result)
    r = run_bass_kernel_spmd(nc, [arrays], core_ids=[0])
    return r.results[0]["out_0"]
```
